# Optimizing a Trainium2 kernel written in Bass

```python
import numpy as np
import jax
import jax.numpy as jnp

def _softmax(x, axis=-1):
    return jax.nn.softmax(x, axis=axis)

def _gelu(x):
    return jax.nn.gelu(x, approximate=True)

def _silu(x):
    return jax.nn.silu(x)

def _sigmoid(x):
    return jax.nn.sigmoid(x)

def _layernorm(x, axis=-1, eps=1e-05):
    m = jnp.mean(x, axis=axis, keepdims=True)
    v = jnp.var(x, axis=axis, keepdims=True)
    return (x - m) / jnp.sqrt(v + eps)

def _scatter_add(tgt, idx, src, axis=0):
    return tgt.at[idx].add(src)

def _segment_sum(src, seg, n):
    return jax.ops.segment_sum(src, seg, n)
kernel_name = 'mk_gnn_preln_d2_gnn_r8_898c1d'

def setup_inputs(seed: int=0):
    np.random.seed(seed)
    _w = jnp.asarray

    def _rec_inputs():
        import jax
        import jax.numpy as jnp
        _gk = jax.random.key(seed)
        x = -0.000202 + 1 * jax.random.normal(jax.random.fold_in(_gk, 1), (6250, 128), jnp.float32)
        _s = jax.random.randint(jax.random.fold_in(_gk, 2), (50000,), 0, 6250, jnp.int32)
        _d = jax.random.randint(jax.random.fold_in(_gk, 3), (50000,), 0, 6250, jnp.int32)
        _loop = jnp.arange(6250, dtype=jnp.int32)
        src = jnp.concatenate([_s, _d, _loop])
        dst = jnp.concatenate([_d, _s, _loop])
        _o = jnp.argsort(dst, stable=True)
        src = src[_o]
        dst = dst[_o]
        edge_attr_128 = 9.41057e-06 + 1 * jax.random.normal(jax.random.fold_in(_gk, 12), (106250, 128), jnp.float32)
        return (x, src, dst, edge_attr_128)
    x, src, dst, edge_attr_128 = _rec_inputs()

    def _L0_gnn_setup():
        import jax, jax.numpy as jnp
        import numpy as np
        N_NODES = 6250
        N_EDGES = 100000
        C = 128
        key = jax.random.key(seed)
        k1, k2, k3, k4 = jax.random.split(key, 4)
        x = jax.random.normal(k1, (N_NODES, C), dtype=jnp.float32)
        W = jax.random.normal(k2, (C, 2 * C), dtype=jnp.float32) * (1.0 / np.sqrt(2 * C))
        b = jax.random.normal(k3, (C,), dtype=jnp.float32) * 0.01
        edge_index = jax.random.randint(k4, (2, N_EDGES), 0, N_NODES, dtype=jnp.int32)
        return {'x': x, 'W': W, 'b': b, 'edge_index': edge_index}
    _L0_gnn_all = _L0_gnn_setup()
    _L0_gnn_in = {k: v for k, v in _L0_gnn_all.items() if k in ('W', 'b')}
    del _L0_gnn_all

    def _L1_gnn_setup():
        import jax, jax.numpy as jnp
        import numpy as np
        N_NODES = 12500
        N_EDGES = 200000
        N_GRAPHS = 64
        D_X = 128
        D_E = 128
        D_U = 128
        HIDDEN = 128
        OUT = 128
        IN_SIZE = D_X + D_E + D_U
        key = jax.random.key(seed)
        ks = jax.random.split(key, 10)
        x = jax.random.normal(ks[0], (N_NODES, D_X), dtype=jnp.float32)
        edge_index = jax.random.randint(ks[1], (2, N_EDGES), 0, N_NODES, dtype=jnp.int64)
        edge_attr = jax.random.normal(ks[2], (N_EDGES, D_E), dtype=jnp.float32)
        u = jax.random.normal(ks[3], (N_GRAPHS, D_U), dtype=jnp.float32)
        batch = jnp.sort(jax.random.randint(ks[4], (N_NODES,), 0, N_GRAPHS, dtype=jnp.int64))
        W1 = jax.random.normal(ks[5], (IN_SIZE, HIDDEN), dtype=jnp.float32) * (1.0 / np.sqrt(IN_SIZE))
        b1 = jnp.zeros((HIDDEN,), dtype=jnp.float32)
        W2 = jax.random.normal(ks[6], (HIDDEN, HIDDEN), dtype=jnp.float32) * (1.0 / np.sqrt(HIDDEN))
        b2 = jnp.zeros((HIDDEN,), dtype=jnp.float32)
        W3 = jax.random.normal(ks[7], (HIDDEN, OUT), dtype=jnp.float32) * (1.0 / np.sqrt(HIDDEN))
        b3 = jnp.zeros((OUT,), dtype=jnp.float32)
        return {'x': x, 'edge_index': edge_index, 'edge_attr': edge_attr, 'u': u, 'batch': batch, 'W1': W1, 'b1': b1, 'W2': W2, 'b2': b2, 'W3': W3, 'b3': b3}
    _L1_gnn_all = _L1_gnn_setup()
    _L1_gnn_in = {k: v for k, v in _L1_gnn_all.items() if k in ('u', 'W1', 'b1', 'W2', 'b2', 'W3', 'b3')}
    del _L1_gnn_all
    return {'x': x, 'src': src, 'dst': dst, 'edge_attr_128': edge_attr_128, 'L0_gnn_W': _L0_gnn_in['W'], 'L0_gnn_b': _L0_gnn_in['b'], 'L1_gnn_u': _L1_gnn_in['u'], 'L1_gnn_W1': _L1_gnn_in['W1'], 'L1_gnn_b1': _L1_gnn_in['b1'], 'L1_gnn_W2': _L1_gnn_in['W2'], 'L1_gnn_b2': _L1_gnn_in['b2'], 'L1_gnn_W3': _L1_gnn_in['W3'], 'L1_gnn_b3': _L1_gnn_in['b3']}

def reference(x, src, dst, edge_attr_128, L0_gnn_W, L0_gnn_b, L1_gnn_u, L1_gnn_W1, L1_gnn_b1, L1_gnn_W2, L1_gnn_b2, L1_gnn_W3, L1_gnn_b3):
    import jax
    import jax.numpy as jnp

    def _L0_gnn_ref(x, W, b, edge_index):
        import jax, jax.numpy as jnp
        import numpy as np
        N_NODES = 6250
        N_EDGES = 100000
        C = 128
        src, dst = (edge_index[0], edge_index[1])
        xi = x[dst]
        xj = x[src]
        feat = jnp.concatenate([xi, xj - xi], axis=-1)
        msg = feat @ W.T + b
        agg = jax.ops.segment_max(msg, dst, num_segments=N_NODES)
        agg = jnp.where(jnp.isfinite(agg), agg, jnp.zeros((), agg.dtype))
        return jax.nn.relu(agg)

    def _L1_gnn_ref(x, edge_index, edge_attr, u, batch, W1, b1, W2, b2, W3, b3):
        import jax, jax.numpy as jnp
        import numpy as np
        N_NODES = 12500
        N_EDGES = 200000
        N_GRAPHS = 64
        D_X = 128
        D_E = 128
        D_U = 128
        HIDDEN = 128
        OUT = 128
        IN_SIZE = D_X + D_E + D_U
        edge_dst = edge_index[1]
        agg = jax.ops.segment_sum(edge_attr, edge_dst, num_segments=x.shape[0])
        model_in = jnp.concatenate([x, agg, u[batch]], axis=1)
        h = jax.nn.relu(model_in @ W1 + b1)
        h = jax.nn.relu(h @ W2 + b2)
        return h @ W3 + b3
    edge_index = jnp.stack([src, dst])
    batch0 = jnp.zeros((6250,), jnp.int32)
    h = jnp.maximum(_layernorm(x, axis=-1), 0.0)
    x = x + _L0_gnn_ref(h, L0_gnn_W, L0_gnn_b, edge_index)
    h = jnp.maximum(_layernorm(x, axis=-1), 0.0)
    x = x + _L1_gnn_ref(h, edge_index, edge_attr_128, L1_gnn_u, batch0, L1_gnn_W1, L1_gnn_b1, L1_gnn_W2, L1_gnn_b2, L1_gnn_W3, L1_gnn_b3)
    return x

_drawn_inputs = setup_inputs


def setup_inputs(seed=0):
    import zlib

    import numpy as np

    out = dict(_drawn_inputs(seed))
    spreads = {'L1_gnn_b1': (0.0, 0.341), 'L1_gnn_b2': (0.0, 0.1), 'L1_gnn_b3': (0.0, 0.1)}
    factors = {'L0_gnn_b': 8.0}
    for name, (base, spread) in spreads.items():
        noise = np.random.default_rng([zlib.crc32(name.encode()), seed]).standard_normal(out[name].shape)
        drawn = base * np.exp(spread * noise) if base else spread * noise
        out[name] = jnp.asarray(drawn.astype(out[name].dtype))
    for name, factor in factors.items():
        out[name] = (out[name] * factor).astype(out[name].dtype)
    return out
```

```python
from contextlib import ExitStack

import numpy as np

import concourse.bass as bass
from concourse import mybir

ALU = mybir.AluOpType
ACT = mybir.ActivationFunctionType
F32 = mybir.dt.float32
BF16 = mybir.dt.bfloat16
I32 = mybir.dt.int32

P = 128
D = 128
BIG = 3.0e38
EPS = 1e-5
CHUNK = 8
SLOTS = 4


def peeled(engine, count):
    yield 0
    with engine.Fori(1, count) as i:
        yield i


def later(i):
    return not (isinstance(i, int) and i == 0)


def gnn_block(nc, x, src, dst, attr, W0, b0, u, W1, b1, W2, b2, W3, b3, out):
    N, E = x.shape[0], attr.shape[0]
    NT = -(-N // P)
    FULL_T = N // P
    TAIL_N = N - FULL_T * P
    GROUP = 7
    NG = NT // GROUP
    HALVES = [(0, 4), (4, 3)]
    assert NT == NG * GROUP and TAIL_N > 0 and FULL_T == NT - 1
    STEPS = -(-(-(-E // P)) // (CHUNK * SLOTS)) * CHUNK * SLOTS
    LAST = E - (P - 1) * STEPS
    assert 0 < LAST < STEPS
    LOOPS = STEPS // (CHUNK * SLOTS)
    PAD_DST = 8191

    with ExitStack() as ctx:
        def sb(name, shape, dt=F32):
            return ctx.enter_context(nc.sbuf_tensor(name, shape, dt))

        def psum(name, shape, dt=F32):
            return ctx.enter_context(nc.psum_tensor(name, shape, dt))

        def sem(name):
            return ctx.enter_context(nc.semaphore(name))

        B_rows = nc.dram_tensor("B_rows", (NT * P, D), F32, kind="Internal").ap()
        run_rows = nc.dram_tensor("run_rows", (P * STEPS, 2 * D), F32, kind="Internal").ap()

        ident = sb("ident", [P, P])
        prefix_u = sb("prefix_u", [P, P])
        ones = sb("ones", [P, P])
        zeros_b = sb("zeros_b", [P, P], BF16)
        iota_i = sb("iota_i", [P, P], I32)
        iota_b = sb("iota_b", [P, P], BF16)
        part_i = sb("part_i", [P, 1], I32)
        part_f = sb("part_f", [P, 1])
        w0 = sb("w0", [P, 2 * D])
        w0T = sb("w0T", [P, 2 * D])
        w1 = sb("w1", [P, 3, D])
        w2 = sb("w2", [P, D])
        w3 = sb("w3", [P, D])
        b0_rows = sb("b0_rows", [P, D])
        b3_row = sb("b3_row", [P, 4 * D])
        b1_col = sb("b1_col", [P, 1])
        b2_col = sb("b2_col", [P, 1])
        eps_col = sb("eps_col", [P, 1])
        u_col = sb("u_col", [P, 1])
        c1_col = sb("c1_col", [P, 1])

        src_t = sb("src_t", [P, STEPS], I32)
        dst_t = sb("dst_t", [P, STEPS], I32)
        tmp_i = sb("tmp_i", [P, STEPS], I32)
        dst_f = sb("dst_f", [P, STEPS])
        keep = sb("keep", [P, STEPS])
        drop = sb("drop", [P, STEPS])
        eq_first = sb("eq_first", [P, STEPS])
        lo_b = sb("lo_b", [P, STEPS], BF16)
        hi_b = sb("hi_b", [P, STEPS], BF16)
        prev_i = sb("prev_i", [P, 1], I32)
        prev_f = sb("prev_f", [P, 1])
        first_n = sb("first_n", [P, 1])
        fix_f = sb("fix_f", [P, 1])
        fix_i = sb("fix_i", [P, 1], I32)
        cont = sb("cont", [P, 1])
        cont_neg = sb("cont_neg", [P, 1])
        through = sb("through", [P, 1])
        diag = sb("diag", [P, P])
        thr_row = sb("thr_row", [P, 2, P])
        carryT = sb("carryT", [P, 2, P])
        runT = sb("runT", [P, 2, P + 1])
        fix = sb("fix", [P, 2 * D])

        X = sb("X", [P, NT, D])
        A = sb("A", [P, NT, D])
        stats = sb("stats", [P, NT, 6])
        x1 = sb("x1", [P, GROUP, D])
        mv = sb("mv", [P, NT, 2])
        std = sb("std", [P, NT])
        rstd = sb("rstd", [P, NT])
        nmr = sb("nmr", [P, NT])
        H = sb("H", [P, GROUP, D])
        hT = sb("hT", [P, GROUP, P])
        Bst = sb("Bst", [P, GROUP, D])
        count = sb("count", [P, NT])
        has = sb("has", [P, NT])
        nothas = sb("nothas", [P, NT])
        tot = sb("tot", [P, NT])
        totscan = sb("totscan", [P, NT])
        end_f = sb("end_f", [P, NT])
        end_i = sb("end_i", [P, NT], I32)

        ring = sb("ring", [P, SLOTS * CHUNK * 4 * D])
        n_run = SLOTS * CHUNK * 2 * D
        n_one = SLOTS * CHUNK * D
        run = ring[:, 0:n_run].rearrange("p (s j d) -> p s j d", s=SLOTS, j=CHUNK)
        gat = ring[:, n_run:n_run + n_one].rearrange("p (s j d) -> p s j d", s=SLOTS, j=CHUNK)
        att = ring[:, n_run + n_one:n_run + 2 * n_one].rearrange("p (s j d) -> p s j d", s=SLOTS, j=CHUNK)
        ends = ring[:, 0:NT * 2 * D].rearrange("p (t d) -> p t d", t=NT)
        idx = sb("idx", [P, SLOTS, CHUNK], I32)
        oh_lo = sb("oh_lo", [P, SLOTS, CHUNK, P], BF16)
        oh_hi = sb("oh_hi", [P, SLOTS, CHUNK, NT], BF16)
        tmpz = sb("tmpz", [P, GROUP, D])
        SM = sb("SM", [P, GROUP, D])
        smT = sb("smT", [P, GROUP, P])
        a1 = sb("a1", [P, GROUP, P])
        a2 = sb("a2", [P, GROUP, P])
        ost = sb("ost", [P, GROUP, D])

        pT = psum("pT", [P, 2, 512])
        pM = psum("pM", [P, 4, 512])
        pH = psum("pH", [P, 512])
        pO = psum("pO", [P, 512])

        x_in = sem("x_in")
        dst_in = sem("dst_in")
        src_in = sem("src_in")
        w_in = sem("w_in")
        pad_set = sem("pad_set")
        const_set = sem("const_set")
        pool_own = sem("pool_own")
        w0_ready = sem("w0_ready")
        w0_turned = sem("w0_turned")
        dve_own = sem("dve_own")
        std_ready = sem("std_ready")
        stat_ready = sem("stat_ready")
        h_ready = [sem(f"h_ready{h}") for h in range(2)]
        t_ready = [sem(f"t_ready{h}") for h in range(2)]
        hT_ready = [sem(f"hT_ready{h}") for h in range(2)]
        ab_ready = [sem(f"ab_ready{h}") for h in range(2)]
        a_taken = [sem(f"a_taken{h}") for h in range(2)]
        b_taken = [sem(f"b_taken{h}") for h in range(2)]
        b_out = [sem(f"b_out{h}") for h in range(2)]
        init_set = sem("init_set")
        idx_ready = [sem(f"idx_ready{s}") for s in range(SLOTS)]
        gathered = [sem(f"gathered{s}") for s in range(SLOTS)]
        attr_in = [sem(f"attr_in{s}") for s in range(SLOTS)]
        rows_out = [sem(f"rows_out{s}") for s in range(SLOTS)]
        max_steps = sem("max_steps")
        sum_steps = sem("sum_steps")
        max_done = [sem(f"max_done{s}") for s in range(SLOTS)]
        sum_done = [sem(f"sum_done{s}") for s in range(SLOTS)]
        onehots = [sem(f"onehots{s}") for s in range(SLOTS)]
        counted = [sem(f"counted{s}") for s in range(SLOTS)]
        hist_done = sem("hist_done")
        count_ready = sem("count_ready")
        prefix_ready = sem("prefix_ready")
        end_ready = sem("end_ready")
        diag_ready = sem("diag_ready")
        thr_ready = sem("thr_ready")
        carry_turned = sem("carry_turned")
        run_ready = sem("run_ready")
        run_turned = sem("run_turned")
        fix_in = sem("fix_in")
        fix_ready = sem("fix_ready")
        fix_out = sem("fix_out")
        end_in = [sem(f"end_in{h}") for h in range(2)]
        var_ready = [sem(f"var_ready{h}") for h in range(2)]
        x1_ready = [sem(f"x1_ready{h}") for h in range(2)]
        sm_ready = [sem(f"sm_ready{h}") for h in range(2)]
        h2_ready = [sem(f"h2_ready{h}") for h in range(2)]
        st_ready = [sem(f"st_ready{h}") for h in range(2)]
        ht_ready = [sem(f"ht_ready{h}") for h in range(2)]
        smT_ready = [sem(f"smT_ready{h}") for h in range(2)]
        h2T_ready = [sem(f"h2T_ready{h}") for h in range(2)]
        l1_ready = [sem(f"l1_ready{h}") for h in range(2)]
        a1_ready = [sem(f"a1_ready{h}") for h in range(2)]
        l2_ready = sem("l2_ready")
        a2_ready = sem("a2_ready")
        l3_ready = sem("l3_ready")
        o_ready = sem("o_ready")
        o_out = [sem(f"o_out{h}") for h in range(2)]

        x_tiles = x[0:FULL_T * P, :].rearrange("(t p) d -> p t d", p=P)
        out_tiles = out[0:FULL_T * P, :].rearrange("(t p) d -> p t d", p=P)
        B_tiles = B_rows.rearrange("(t p) d -> p t d", p=P)
        run_view = run_rows.rearrange("(p k) d -> p k d", p=P)
        LASTP = P - 1
        attr_view = attr[0:LASTP * STEPS, :].rearrange("(p k) d -> p k d", k=STEPS)
        attr_last = attr[LASTP * STEPS:E, :].rearrange("(a k) d -> a k d", a=1)
        MAINP = 112

        def load_edge_ints(eng, table, vec, signal):
            view = vec[0:LASTP * STEPS].rearrange("(p k) -> p k", k=STEPS)
            eng.dma_start(table[0:MAINP, :], view[0:MAINP, :]).then_inc(signal, 16)
            eng.dma_start(table[MAINP:LASTP, :], view[MAINP:LASTP, :]).then_inc(signal, 16)
            eng.dma_start(table[LASTP:P, 0:LAST],
                          vec[LASTP * STEPS:E].rearrange("(a k) -> a k", a=1)).then_inc(signal, 16)

        def tiles(ap, g, h):
            first, n = HALVES[h]
            return ap[:, bass.ds(g * GROUP + first, n), :]

        def ab_rows(h):
            n = HALVES[h][1]
            return pM[:, 2 * h:2 * h + 2, :].rearrange("p a b -> p (a b)")[:, 0:n * 2 * D].rearrange(
                "p (j d) -> p j d", j=n)

        block = ctx.enter_context(nc.Block())

        @block.sync
        def _(sp):
            sp.wait_ge(pad_set, 4)
            load_edge_ints(sp, dst_t, dst, dst_in)
            with nc.allow_non_contiguous_dma(reason="one value per partition"):
                sp.dma_start(prev_i[1:P, :],
                             dst[0:LASTP * STEPS].rearrange("(p k) -> p k", k=STEPS)[:, STEPS - 1:STEPS]
                             ).then_inc(dst_in, 16)
            sp.dma_start(X[:, 0:FULL_T, :], x_tiles).then_inc(x_in, 16)
            sp.dma_start(X[0:TAIL_N, FULL_T, :], x[FULL_T * P:N, :]).then_inc(x_in, 16)

            for g in peeled(sp, NG):
                for h, (first, n) in enumerate(HALVES):
                    sp.wait_ge(b_taken[h], g + 1)
                    sp.dma_start(tiles(B_tiles, g, h), Bst[:, first:first + n, :]).then_inc(b_out[h], 16)

            def load_attr(i, s, last_row, n_last):
                k0 = i * (SLOTS * CHUNK) + s * CHUNK
                if later(i):
                    sp.wait_ge(sum_done[s], i)
                sp.dma_start(att[0:MAINP, s], attr_view[0:MAINP, bass.ds(k0, CHUNK), :]).then_inc(attr_in[s], 16)
                sp.dma_start(att[MAINP:LASTP, s], attr_view[MAINP:LASTP, bass.ds(k0, CHUNK), :]
                             ).then_inc(attr_in[s], 16)
                sp.dma_start(att[LASTP:P, s, 0:n_last], attr_last[:, bass.ds(last_row, n_last), :]
                             ).then_inc(attr_in[s], 16)

            whole = LAST // (SLOTS * CHUNK)
            for i in peeled(sp, whole):
                for s in range(SLOTS):
                    load_attr(i, s, i * (SLOTS * CHUNK) + s * CHUNK, CHUNK)
            for s in range(SLOTS):
                k0 = whole * SLOTS * CHUNK + s * CHUNK
                n_last = max(0, min(CHUNK, LAST - k0))
                load_attr(whole, s, k0 if n_last else 0, n_last or 1)
            with sp.Fori(whole + 1, LOOPS) as i:
                for s in range(SLOTS):
                    load_attr(i, s, 0, 1)

            for g in peeled(sp, NG - 1):
                for h, (first, n) in enumerate(HALVES):
                    sp.wait_ge(o_ready, g * 2 + h + 1)
                    sp.dma_start(tiles(out_tiles, g, h), ost[:, first:first + n, :]).then_inc(o_out[h], 16)
            g = NG - 1
            for h, (first, n) in enumerate(HALVES):
                sp.wait_ge(o_ready, g * 2 + h + 1)
                lo = g * GROUP + first
                n_full = min(n, FULL_T - lo)
                sp.dma_start(out_tiles[:, lo:lo + n_full, :], ost[:, first:first + n_full, :]).then_inc(o_out[h], 16)
            sp.dma_start(out[FULL_T * P:N, :], ost[0:TAIL_N, GROUP - 1, :]).then_inc(o_out[1], 16)
            sp.wait_ge(o_out[0], 16 * NG)
            sp.wait_ge(o_out[1], 16 * (NG + 1))

        @block.gpsimd
        def _(pool):
            pool.memset(ones[:], 1.0).then_inc(const_set, 1)
            pool.iota(iota_i[:], [[1, P]], base=0, channel_multiplier=0).then_inc(const_set, 1)
            pool.iota(part_i[:], [[0, 1]], base=0, channel_multiplier=STEPS).then_inc(const_set, 1)
            pool.wait_ge(const_set, 3)
            pool.affine_select(out=ident[:], in_=ones[:], compare_op=ALU.is_equal, fill=0.0, base=0,
                               pattern=[[-1, P]], channel_multiplier=1).then_inc(const_set, 1)
            pool.affine_select(out=prefix_u[:], in_=ones[:], compare_op=ALU.is_ge, fill=0.0, base=0,
                               pattern=[[1, P]], channel_multiplier=-1).then_inc(const_set, 1)

            for h in range(2):
                pool.wait_ge(b_out[h], 16 * NG)

            for i in peeled(pool, LOOPS):
                for s in range(SLOTS):
                    pool.wait_ge(idx_ready[s], i + 1)
                    if later(i):
                        pool.wait_ge(max_done[s], i)
                    pool.nop(nofuse=True)
                    for j in range(CHUNK):
                        pool.indirect_dma_start(
                            gat[:, s, j, :], None, B_rows,
                            bass.IndirectOffsetOnAxis(ap=idx[:, s, j:j + 1], axis=0)).then_inc(gathered[s], 16)

            pool.wait_ge(fix_ready, 1)
            for s in range(SLOTS):
                pool.wait_ge(rows_out[s], 16 * LOOPS)
            pool.indirect_dma_start(fix[:], None, run_rows,
                                    bass.IndirectOffsetOnAxis(ap=fix_i[:], axis=0)).then_inc(fix_in, 16)
            pool.wait_ge(fix_ready, 3)
            pool.indirect_dma_start(run_rows, bass.IndirectOffsetOnAxis(ap=fix_i[:], axis=0),
                                    fix[:], None).then_inc(fix_out, 16)

            pool.wait_ge(end_ready, 1)
            pool.wait_ge(fix_out, 16)
            pool.wait_ge(run_turned, 1)
            for g in range(NG):
                for h, (first, n) in enumerate(HALVES):
                    if later(g):
                        pool.wait_ge(end_in[h], 16 * n * g)
                    for t in range(g * GROUP + first, g * GROUP + first + n):
                        pool.indirect_dma_start(
                            ends[:, t, :], None, run_rows,
                            bass.IndirectOffsetOnAxis(ap=end_i[:, t:t + 1], axis=0)).then_inc(end_in[h], 16)

        @block.scalar
        def _(act):
            w_loads = [
                (w0[:], W0), (w1[:], W1.rearrange("(c k) m -> k c m", k=P)), (w2[:], W2), (w3[:], W3),
                (b1_col[:], b1.rearrange("(k a) -> k a", a=1)), (b2_col[:], b2.rearrange("(k a) -> k a", a=1)),
                (u_col[:], u[0:1, :].rearrange("a k -> k a")),
                (b0_rows[:], b0.rearrange("(a k) -> a k", a=1).to_broadcast([P, D])),
                (b3_row[0:1, :].rearrange("a (r k) -> a r k", r=4),
                 b3.rearrange("(a r k) -> a r k", a=1, r=1).to_broadcast([1, 4, D])),
            ]
            with nc.allow_non_contiguous_dma(reason="columns of 128 values"):
                for to, what in w_loads:
                    act.dma_start(to, what).then_inc(w_in, 16)
            act.wait_ge(pad_set, 4)
            load_edge_ints(act, src_t, src, src_in)

            act.wait_ge(dve_own, 8)
            act.activation(std[:], mv[:, :, 1], ACT.Sqrt, bias=eps_col[:]).then_inc(std_ready, 1)
            act.wait_ge(stat_ready, 1)
            act.wait_ge(x_in, 32)
            for g in peeled(act, NG):
                for h, (first, n) in enumerate(HALVES):
                    if later(g):
                        act.wait_ge(t_ready[h], g)
                    for j in range(first, first + n):
                        t = g * GROUP + j
                        ins = act.activation(H[:, j:j + 1, :], X[:, bass.ds(t, 1), :], ACT.Relu,
                                             bias=nmr[:, bass.ds(t, 1)], scale=rstd[:, bass.ds(t, 1)])
                        if j == first + n - 1:
                            ins.then_inc(h_ready[h], 1)
                for h, (first, n) in enumerate(HALVES):
                    act.wait_ge(ab_ready[h], g + 1)
                    if later(g):
                        act.wait_ge(b_out[h], g * 16)
                    act.activation(Bst[:, first:first + n, :], ab_rows(h)[:, :, 0:D], ACT.Copy).then_inc(b_taken[h], 1)

            act.wait_ge(src_in, 48)
            for s in range(SLOTS):
                act.activation(idx[:, s, :], src_t[:, s * CHUNK:(s + 1) * CHUNK], ACT.Copy).then_inc(idx_ready[s], 1)

            def store_rows(i, s):
                act.wait_ge(max_done[s], i + 1)
                act.wait_ge(sum_done[s], i + 1)
                act.dma_start(run_view[:, bass.ds(i * (SLOTS * CHUNK) + s * CHUNK, CHUNK), :],
                              run[:, s]).then_inc(rows_out[s], 16)

            for i in peeled(act, LOOPS - 1):
                for s in range(SLOTS):
                    store_rows(i, s)
                    act.wait_ge(gathered[s], i * (16 * CHUNK) + 16 * CHUNK)
                    act.activation(idx[:, s, :],
                                   src_t[:, bass.ds(i * (SLOTS * CHUNK) + (SLOTS + s) * CHUNK, CHUNK)],
                                   ACT.Copy).then_inc(idx_ready[s], 1)
            for s in range(SLOTS):
                store_rows(LOOPS - 1, s)

            act.wait_ge(end_ready, 1)
            for g in peeled(act, NG):
                for h, (first, n) in enumerate(HALVES):
                    act.wait_ge(end_in[h], g * (16 * n) + 16 * n)
                    if later(g):
                        act.wait_ge(st_ready[h], g)
                    for j in range(first, first + n):
                        t = g * GROUP + j
                        ins = act.activation(SM[:, j:j + 1, :], ends[:, bass.ds(t, 1), D:2 * D], ACT.Copy,
                                             scale=has[:, bass.ds(t, 1)])
                        if j == first + n - 1:
                            ins.then_inc(sm_ready[h], 1)
                for h, (first, n) in enumerate(HALVES):
                    ts = slice(first, first + n)
                    act.wait_ge(var_ready[h], g + 1)
                    act.activation(std[:, ts], mv[:, ts, 1], ACT.Sqrt, bias=eps_col[:]).then_inc(std_ready, 1)
                for h, (first, n) in enumerate(HALVES):
                    act.wait_ge(x1_ready[h], g + 1)
                    if later(g):
                        act.wait_ge(ht_ready[h], g)
                    for j in range(first, first + n):
                        ins = act.activation(H[:, j, :], x1[:, j, :], ACT.Relu,
                                             bias=nmr[:, j:j + 1], scale=rstd[:, j:j + 1])
                        if j == first + n - 1:
                            ins.then_inc(h2_ready[h], 1)
                    act.wait_ge(st_ready[h], g + 1)
                    if later(g):
                        act.wait_ge(l1_ready[h], g)
                    act.activation(smT[:, first:first + n, :], pM[:, h, 0:n * P].rearrange("p (j q) -> p j q", j=n),
                                   ACT.Copy).then_inc(smT_ready[h], 1)
                for h, (first, n) in enumerate(HALVES):
                    act.wait_ge(l1_ready[h], g + 1)
                    if later(g):
                        act.wait_ge(l2_ready, g * 2)
                    act.activation(a1[:, first:first + n, :],
                                   pM[:, 2 + h, 0:n * P].rearrange("p (j q) -> p j q", j=n),
                                   ACT.Relu, bias=c1_col[:]).then_inc(a1_ready[h], 1)

        @block.tensor
        def _(pe):
            pe.wait_ge(const_set, 5)
            pe.wait_ge(w_in, 16 * 9)
            pe.transpose(pO[:, 0:P], w0[:, 0:D], ident[:])
            pe.transpose(pO[:, P:2 * P], w0[:, D:2 * D], ident[:])
            pe.matmul(pO[:, 256:257], w1[:, 2, :], u_col[:], start=True, stop=True).then_inc(w0_turned, 1)
            pe.wait_ge(init_set, 1)
            pe.matmul(pH[:, 0:NT], zeros_b[:], zeros_b[:, 0:NT], start=True, stop=False, skip_group_check=True)

            pe.wait_ge(w0_ready, 2)
            for g in peeled(pe, NG):
                for h, (first, n) in enumerate(HALVES):
                    pe.wait_ge(h_ready[h], g + 1)
                    if later(g):
                        pe.wait_ge(hT_ready[h], g)
                    for j in range(n):
                        mm = pe.transpose(pT[:, h, j * P:(j + 1) * P], H[:, first + j, :], ident[:])
                    mm.then_inc(t_ready[h], 1)
                for h, (first, n) in enumerate(HALVES):
                    pe.wait_ge(hT_ready[h], g + 1)
                    if later(g):
                        pe.wait_ge(a_taken[h], g)
                    if later(g):
                        pe.wait_ge(b_taken[h], g)
                    for j in range(n):
                        mm = pe.matmul(ab_rows(h)[:, j, :], hT[:, first + j, :], w0T[:], start=True, stop=True)
                    mm.then_inc(ab_ready[h], 1)

            for i in peeled(pe, LOOPS):
                for s in range(SLOTS):
                    pe.wait_ge(onehots[s], i * 2 + 2)
                    for j in range(CHUNK):
                        mm = pe.matmul(pH[:, 0:NT], oh_lo[:, s, j, :], oh_hi[:, s, j, :], start=False, stop=False,
                                       skip_group_check=True)
                    mm.then_inc(counted[s], 1)
            pe.matmul(pH[:, 0:NT], zeros_b[:], zeros_b[:, 0:NT], start=False, stop=True,
                      skip_group_check=True).then_inc(hist_done, 1)

            pe.wait_ge(diag_ready, 1)
            pe.matmul(pT[:, 1, 0:P], ones[:], diag[:], start=True, stop=True).then_inc(thr_ready, 1)
            pe.wait_ge(max_done[SLOTS - 1], LOOPS)
            pe.wait_ge(sum_done[SLOTS - 1], LOOPS)
            pe.transpose(pT[:, 0, 0:P], run[:, SLOTS - 1, CHUNK - 1, 0:D], ident[:])
            pe.transpose(pT[:, 0, P:2 * P], run[:, SLOTS - 1, CHUNK - 1, D:2 * D], ident[:]).then_inc(carry_turned, 1)
            pe.wait_ge(run_ready, 2)
            pe.transpose(pM[:, 0, 0:P], runT[:, 0, 0:P], ident[:])
            pe.transpose(pM[:, 0, P:2 * P], runT[:, 1, 0:P], ident[:]).then_inc(run_turned, 1)
            pe.wait_ge(count_ready, 1)
            pe.matmul(pO[:, 0:NT], prefix_u[:], count[:], start=True, stop=True)
            pe.matmul(pO[:, NT:2 * NT], ones[:], count[:], start=True, stop=True).then_inc(prefix_ready, 1)
            pe.wait_ge(fix_ready, 3)

            for g in peeled(pe, NG):
                for h, (first, n) in enumerate(HALVES):
                    pe.wait_ge(sm_ready[h], g + 1)
                    if later(g):
                        pe.wait_ge(smT_ready[h], g)
                    for j in range(n):
                        mm = pe.transpose(pM[:, h, j * P:(j + 1) * P], SM[:, first + j, :], ident[:])
                    mm.then_inc(st_ready[h], 1)
                for h, (first, n) in enumerate(HALVES):
                    pe.wait_ge(h2_ready[h], g + 1)
                    if later(g):
                        pe.wait_ge(h2T_ready[h], g)
                    for j in range(n):
                        mm = pe.transpose(pT[:, h, j * P:(j + 1) * P], H[:, first + j, :], ident[:])
                    mm.then_inc(ht_ready[h], 1)
                for h, (first, n) in enumerate(HALVES):
                    pe.wait_ge(smT_ready[h], g + 1)
                    pe.wait_ge(h2T_ready[h], g + 1)
                    if later(g):
                        pe.wait_ge(a1_ready[h], g)
                    o = pM[:, 2 + h, 0:n * P].rearrange("p (j q) -> p j q", j=n)
                    pe.matmul(o, w1[:, 0, :], hT[:, first:first + n, :], start=True, stop=False)
                    pe.matmul(o, w1[:, 1, :], smT[:, first:first + n, :], start=False, stop=True
                              ).then_inc(l1_ready[h], 1)
                for h, (first, n) in enumerate(HALVES):
                    pe.wait_ge(a1_ready[h], g + 1)
                    if later(g) or h:
                        pe.wait_ge(a2_ready, g * 2 + h)
                    pe.matmul(pH[:, 0:n * P].rearrange("p (j q) -> p j q", j=n), w2[:], a1[:, first:first + n, :],
                              start=True, stop=True).then_inc(l2_ready, 1)
                    if later(g) or h:
                        pe.wait_ge(o_ready, g * 2 + h)
                    pe.matmul(pO[:, 0:n * P], ones[0:1, :], b3_row[0:1, 0:n * P], start=True, stop=False,
                              skip_group_check=True)
                    pe.wait_ge(a2_ready, g * 2 + h + 1)
                    for j in range(n):
                        mm = pe.matmul(pO[:, j * P:(j + 1) * P], a2[:, first + j, :], w3[:], start=False,
                                       stop=(j == n - 1), skip_group_check=True)
                    mm.then_inc(l3_ready, 1)

        @block.vector
        def _(dve):
            dve.memset(dst_t[96:P, LAST:STEPS], PAD_DST).then_inc(pad_set, 1)
            dve.memset(src_t[96:P, LAST:STEPS], 0).then_inc(pad_set, 1)
            dve.memset(X[96:P, FULL_T, :], 0.0).then_inc(pad_set, 1)
            dve.memset(prev_i[:], -1).then_inc(pad_set, 1)
            dve.memset(eps_col[:], EPS).then_inc(dve_own, 1)
            dve.memset(zeros_b[:], 0.0).then_inc(init_set, 1)
            dve.memset(run[:, SLOTS - 1, CHUNK - 1, 0:D], -BIG).then_inc(dve_own, 1)
            dve.memset(run[:, SLOTS - 1, CHUNK - 1, D:2 * D], 0.0).then_inc(dve_own, 1)
            dve.memset(runT[:, :, 0:1], 0.0).then_inc(dve_own, 1)
            dve.wait_ge(const_set, 5)
            dve.tensor_copy(iota_b[:], iota_i[:]).then_inc(dve_own, 1)
            dve.tensor_copy(part_f[:], part_i[:]).then_inc(dve_own, 1)

            dve.wait_ge(x_in, 32)
            for t in range(NT):
                ins = dve.bn_stats(stats[:, t, :], X[:, t, :])
            ins.then_inc(dve_own, 1)
            dve.wait_ge(dve_own, 7)
            for t in range(NT):
                ins = dve.bn_aggr(mv[:, t, :], stats[:, t, :])
            ins.then_inc(dve_own, 1)
            own = 8
            dve.wait_ge(dve_own, own)
            dve.wait_ge(std_ready, 1)
            dve.reciprocal(rstd[:], std[:]).then_inc(dve_own, 1)
            dve.wait_ge(dve_own, own + 1)
            dve.scalar_tensor_tensor(out=nmr[:], in0=mv[:, :, 0], scalar=-1.0, in1=rstd[:], op0=ALU.mult,
                                     op1=ALU.mult).then_inc(stat_ready, 1)
            own += 1

            dve.wait_ge(w0_turned, 1)
            dve.tensor_copy(w0T[:, 0:D], pO[:, P:2 * P]).then_inc(w0_ready, 1)
            dve.wait_ge(w0_ready, 1)
            dve.tensor_tensor(w0T[:, D:2 * D], pO[:, 0:P], w0T[:, 0:D], ALU.subtract).then_inc(w0_ready, 1)
            dve.tensor_tensor(c1_col[:], pO[:, 256:257], b1_col[:], ALU.add).then_inc(dve_own, 1)
            own += 1

            for g in peeled(dve, NG):
                for h, (first, n) in enumerate(HALVES):
                    dve.wait_ge(t_ready[h], g + 1)
                    if later(g):
                        dve.wait_ge(ab_ready[h], g)
                    dve.tensor_copy(hT[:, first:first + n, :], pT[:, h, 0:n * P].rearrange("p (j q) -> p j q", j=n)
                                    ).then_inc(hT_ready[h], 1)
                for h, (first, n) in enumerate(HALVES):
                    dve.wait_ge(b_taken[h], g + 1)
                    bias = b0_rows[:].rearrange("p (a d) -> p a d", a=1).to_broadcast([P, n, D])
                    dve.tensor_tensor(tiles(A, g, h), ab_rows(h)[:, :, D:2 * D], bias, ALU.add
                                      ).then_inc(a_taken[h], 1)

            dve.wait_ge(dst_in, 64)
            dve.tensor_copy(dst_f[:], dst_t[:]).then_inc(dve_own, 1)
            dve.tensor_scalar(tmp_i[:], dst_t[:], 7, None, ALU.logical_shift_right).then_inc(dve_own, 1)
            dve.memset(keep[:, 0:1], 0.0).then_inc(dve_own, 1)
            dve.wait_ge(dve_own, own + 3)
            dve.tensor_tensor(keep[:, 1:STEPS], dst_f[:, 1:STEPS], dst_f[:, 0:STEPS - 1], ALU.is_equal
                              ).then_inc(dve_own, 1)
            dve.tensor_copy(hi_b[:], tmp_i[:]).then_inc(dve_own, 1)
            dve.wait_ge(dve_own, own + 5)
            dve.tensor_scalar(drop[:], keep[:], 1.0, BIG, ALU.subtract, ALU.mult).then_inc(dve_own, 1)
            dve.tensor_scalar(tmp_i[:], dst_t[:], P - 1, None, ALU.bitwise_and).then_inc(dve_own, 1)
            dve.wait_ge(dve_own, own + 7)
            dve.tensor_copy(lo_b[:], tmp_i[:]).then_inc(dve_own, 1)
            own += 8
            dve.wait_ge(dve_own, own)

            dve.tensor_copy(prev_f[:], prev_i[:]).then_inc(dve_own, 1)
            dve.tensor_scalar(eq_first[:], dst_f[:], dst_f[:, 0:1], None, ALU.is_equal).then_inc(dve_own, 1)
            dve.wait_ge(dve_own, own + 2)
            dve.tensor_scalar(cont[:], prev_f[:], dst_f[:, 0:1], None, ALU.is_equal).then_inc(dve_own, 1)
            dve.tensor_reduce(first_n[:], eq_first[:], mybir.AxisListType.X, ALU.add).then_inc(dve_own, 1)
            dve.wait_ge(dve_own, own + 4)
            dve.scalar_tensor_tensor(out=fix_f[:], in0=first_n[:], scalar=-1.0, in1=part_f[:], op0=ALU.add,
                                     op1=ALU.add).then_inc(dve_own, 1)
            dve.tensor_scalar(through[:], first_n[:], float(STEPS), cont[:, 0:1], ALU.is_equal, ALU.mult
                              ).then_inc(dve_own, 1)
            dve.tensor_scalar(cont_neg[:], cont[:], 1.0, BIG, ALU.subtract, ALU.mult).then_inc(dve_own, 1)
            dve.wait_ge(dve_own, own + 7)
            dve.tensor_copy(fix_i[:], fix_f[:]).then_inc(fix_ready, 1)
            dve.tensor_scalar(diag[:], ident[:], through[:, 0:1], None, ALU.mult).then_inc(diag_ready, 1)
            own += 7

            for i in peeled(dve, LOOPS):
                for s in range(SLOTS):
                    k0 = i * (SLOTS * CHUNK) + s * CHUNK
                    if later(i):
                        dve.wait_ge(counted[s], i)
                    dve.tensor_tensor(
                        oh_lo[:, s], iota_b[:].rearrange("p (a q) -> p a q", a=1).to_broadcast([P, CHUNK, P]),
                        lo_b[:, bass.ds(k0, CHUNK)].rearrange("p (k a) -> p k a", a=1).to_broadcast([P, CHUNK, P]),
                        ALU.is_equal).then_inc(onehots[s], 1)
                    dve.tensor_tensor(
                        oh_hi[:, s], iota_b[:, 0:NT].rearrange("p (a q) -> p a q", a=1).to_broadcast([P, CHUNK, NT]),
                        hi_b[:, bass.ds(k0, CHUNK)].rearrange("p (k a) -> p k a", a=1).to_broadcast([P, CHUNK, NT]),
                        ALU.is_equal).then_inc(onehots[s], 1)
                    dve.wait_ge(gathered[s], i * (16 * CHUNK) + 16 * CHUNK)
                    dve.wait_ge(attr_in[s], i * 48 + 48)
                    if later(i):
                        dve.wait_ge(rows_out[s], i * 16)
                    for j in range(CHUNK):
                        to = run[:, s, j]
                        was = run[:, s, j - 1] if j else run[:, (s - 1) % SLOTS, CHUNK - 1]
                        if j:
                            dve.wait_ge(max_steps, i * (SLOTS * (CHUNK - 1)) + s * (CHUNK - 1) + j)
                        else:
                            if later(i) or s:
                                dve.wait_ge(max_done[s - 1], i + 1 if s else i)
                        ins = dve.scalar_tensor_tensor(
                            out=to[:, 0:D], in0=was[:, 0:D], scalar=drop[:, bass.ds(k0 + j, 1)],
                            in1=gat[:, s, j, :], op0=ALU.add, op1=ALU.max)
                        if j < CHUNK - 1:
                            ins.then_inc(max_steps, 1)
                        else:
                            ins.then_inc(max_done[s], 1)
                        if j:
                            dve.wait_ge(sum_steps, i * (SLOTS * (CHUNK - 1)) + s * (CHUNK - 1) + j)
                        else:
                            if later(i) or s:
                                dve.wait_ge(sum_done[s - 1], i + 1 if s else i)
                        ins = dve.scalar_tensor_tensor(
                            out=to[:, D:2 * D], in0=was[:, D:2 * D], scalar=keep[:, bass.ds(k0 + j, 1)],
                            in1=att[:, s, j, :], op0=ALU.mult, op1=ALU.add)
                        if j < CHUNK - 1:
                            ins.then_inc(sum_steps, 1)
                        else:
                            ins.then_inc(sum_done[s], 1)

            dve.wait_ge(thr_ready, 1)
            dve.tensor_copy(thr_row[:, 1, :], pT[:, 1, 0:P]).then_inc(dve_own, 1)
            dve.tensor_scalar(thr_row[:, 0, :], pT[:, 1, 0:P], 1.0, BIG, ALU.subtract, ALU.mult).then_inc(dve_own, 1)
            dve.wait_ge(carry_turned, 1)
            dve.wait_ge(dve_own, own + 2)
            dve.tensor_tensor_scan(out=runT[:, 0, 1:P + 1], data0=thr_row[:, 0, :], data1=pT[:, 0, 0:P],
                                   initial=-BIG, op0=ALU.add, op1=ALU.max).then_inc(run_ready, 1)
            dve.tensor_tensor_scan(out=runT[:, 1, 1:P + 1], data0=thr_row[:, 1, :], data1=pT[:, 0, P:2 * P],
                                   initial=0.0, op0=ALU.mult, op1=ALU.add).then_inc(run_ready, 1)
            own += 2

            dve.wait_ge(hist_done, 1)
            dve.tensor_copy(count[:], pH[:, 0:NT]).then_inc(count_ready, 1)
            dve.wait_ge(prefix_ready, 1)
            dve.wait_ge(count_ready, 1)
            dve.tensor_scalar(has[:], count[:], 0.5, None, ALU.is_gt).then_inc(dve_own, 1)
            dve.tensor_copy(tot[:], pO[:, NT:2 * NT]).then_inc(dve_own, 1)
            dve.wait_ge(dve_own, own + 2)
            dve.tensor_scalar(nothas[:], has[:], 1.0, BIG, ALU.subtract, ALU.mult).then_inc(dve_own, 1)
            dve.memset(end_f[:], 0.0).then_inc(dve_own, 1)
            dve.wait_ge(dve_own, own + 4)
            dve.tensor_tensor_scan(out=totscan[:], data0=tot[:], data1=end_f[:], initial=0.0, op0=ALU.add,
                                   op1=ALU.add).then_inc(dve_own, 1)
            dve.wait_ge(dve_own, own + 5)
            dve.tensor_tensor(end_f[:], totscan[:], tot[:], ALU.subtract).then_inc(dve_own, 1)
            dve.wait_ge(dve_own, own + 6)
            dve.scalar_tensor_tensor(out=totscan[:], in0=pO[:, 0:NT], scalar=-1.0, in1=end_f[:], op0=ALU.add,
                                     op1=ALU.add).then_inc(dve_own, 1)
            dve.wait_ge(dve_own, own + 7)
            dve.tensor_scalar(end_i[:], totscan[:], 0.0, None, ALU.max).then_inc(end_ready, 1)
            own += 7

            dve.wait_ge(run_turned, 1)
            dve.wait_ge(fix_in, 16)
            dve.scalar_tensor_tensor(out=fix[:, 0:D], in0=pM[:, 0, 0:P], scalar=cont_neg[:, 0:1], in1=fix[:, 0:D],
                                     op0=ALU.add, op1=ALU.max).then_inc(fix_ready, 1)
            dve.scalar_tensor_tensor(out=fix[:, D:2 * D], in0=pM[:, 0, P:2 * P], scalar=cont[:, 0:1],
                                     in1=fix[:, D:2 * D], op0=ALU.mult, op1=ALU.add).then_inc(fix_ready, 1)

            for g in peeled(dve, NG):
                for h, (first, n) in enumerate(HALVES):
                    dve.wait_ge(end_in[h], g * (16 * n) + 16 * n)
                    base = own + g * 8 + 3 * h
                    if later(g):
                        dve.wait_ge(h2_ready[h], g)
                    for j in range(first, first + n):
                        t = bass.ds(g * GROUP + j, 1)
                        ins = dve.scalar_tensor_tensor(out=tmpz[:, j:j + 1, :], in0=ends[:, t, 0:D],
                                                       scalar=nothas[:, t], in1=A[:, t, :], op0=ALU.add, op1=ALU.add)
                    ins.then_inc(dve_own, 1)
                    dve.wait_ge(dve_own, base + 1)
                    dve.scalar_tensor_tensor(out=x1[:, first:first + n, :], in0=tmpz[:, first:first + n, :], scalar=0.0,
                                             in1=tiles(X, g, h), op0=ALU.max, op1=ALU.add).then_inc(dve_own, 1)
                    dve.wait_ge(dve_own, base + 2)
                    for j in range(first, first + n):
                        ins = dve.bn_stats(stats[:, j, :], x1[:, j, :])
                    ins.then_inc(dve_own, 1)
                    dve.wait_ge(dve_own, base + 3)
                    dve.nop(nofuse=True)
                    for j in range(first, first + n):
                        ins = dve.bn_aggr(mv[:, j, :], stats[:, j, :])
                    ins.then_inc(var_ready[h], 1)
                for h, (first, n) in enumerate(HALVES):
                    ts = slice(first, first + n)
                    dve.wait_ge(std_ready, g * 2 + h + 2)
                    dve.reciprocal(rstd[:, ts], std[:, ts]).then_inc(dve_own, 1)
                    dve.wait_ge(dve_own, own + g * 8 + 7 + h)
                    dve.scalar_tensor_tensor(out=nmr[:, ts], in0=mv[:, ts, 0], scalar=-1.0, in1=rstd[:, ts],
                                             op0=ALU.mult, op1=ALU.mult).then_inc(x1_ready[h], 1)
                for h, (first, n) in enumerate(HALVES):
                    dve.wait_ge(ht_ready[h], g + 1)
                    if later(g):
                        dve.wait_ge(l1_ready[h], g)
                    dve.tensor_copy(hT[:, first:first + n, :], pT[:, h, 0:n * P].rearrange("p (j q) -> p j q", j=n)
                                    ).then_inc(h2T_ready[h], 1)
                for h, (first, n) in enumerate(HALVES):
                    dve.wait_ge(l2_ready, g * 2 + h + 1)
                    if later(g):
                        dve.wait_ge(l3_ready, g * 2)
                    dve.tensor_scalar(a2[:, first:first + n, :], pH[:, 0:n * P].rearrange("p (j q) -> p j q", j=n),
                                      b2_col[:, 0:1], 0.0, ALU.add, ALU.max).then_inc(a2_ready, 1)
                    dve.wait_ge(l3_ready, g * 2 + h + 1)
                    if later(g):
                        dve.wait_ge(o_out[h], g * 16)
                    dve.tensor_tensor(ost[:, first:first + n, :], pO[:, 0:n * P].rearrange("p (j q) -> p j q", j=n),
                                      x1[:, first:first + n, :], ALU.add).then_inc(o_ready, 1)


_NAMES = ['x', 'src', 'dst', 'edge_attr_128', 'L0_gnn_W', 'L0_gnn_b', 'L1_gnn_u', 'L1_gnn_W1', 'L1_gnn_b1',
          'L1_gnn_W2', 'L1_gnn_b2', 'L1_gnn_W3', 'L1_gnn_b3']


def kernel(**inputs):
    import concourse.bacc as bacc
    from concourse.bass_utils import run_bass_kernel_spmd

    nc = bacc.Bacc("TRN2", target_bir_lowering=False, num_devices=1)
    arrays = {f"{n}_dram": np.ascontiguousarray(inputs[n]) for n in _NAMES}
    args = [nc.dram_tensor(n, a.shape, mybir.dt.from_np(a.dtype), kind="ExternalInput").ap()
            for n, a in arrays.items()]
    out = nc.dram_tensor("out_dram", tuple(inputs['x'].shape), F32, kind="ExternalOutput").ap()
    gnn_block(nc, *args, out)
    return run_bass_kernel_spmd(nc, [arrays], core_ids=[0]).results[0]["out_dram"]
```

```python
from contextlib import ExitStack

import numpy as np

import concourse.bass as bass
from concourse import mybir

ALU = mybir.AluOpType
ACT = mybir.ActivationFunctionType
F32 = mybir.dt.float32
BF16 = mybir.dt.bfloat16
I32 = mybir.dt.int32

P = 128
D = 128
BIG = 3.0e38
EPS = 1e-5
CHUNK = 8
SLOTS = 4


def peeled(engine, count):
    yield 0
    with engine.Fori(1, count) as i:
        yield i


def later(i):
    return not (isinstance(i, int) and i == 0)


def pipeline(engine, groups, tick, before, after):
    first = -(-after // 2)
    last = groups - -(-before // 2)
    for u in range(-before, 2 * first):
        tick(u // 2, u % 2)
    with engine.Fori(first, last) as g:
        for h in range(2):
            tick(g, h)
    for u in range(2 * last, 2 * groups + after):
        tick(u // 2, u % 2)


def unit(g, h, ahead, groups):
    g, h = g + (h + ahead) // 2, (h + ahead) % 2
    return None if isinstance(g, int) and not 0 <= g < groups else (g, h)


def gnn_block(nc, x, src, dst, attr, W0, b0, u, W1, b1, W2, b2, W3, b3, out):
    N, E = x.shape[0], attr.shape[0]
    NT = -(-N // P)
    FULL_T = N // P
    TAIL_N = N - FULL_T * P
    GROUP = 7
    NG = NT // GROUP
    HALVES = [(0, 4), (4, 3)]
    assert NT == NG * GROUP and TAIL_N > 0 and FULL_T == NT - 1
    STEPS = -(-(-(-E // P)) // (CHUNK * SLOTS)) * CHUNK * SLOTS
    LAST = E - (P - 1) * STEPS
    assert 0 < LAST < STEPS
    LOOPS = STEPS // (CHUNK * SLOTS)
    PAD_DST = 8191

    with ExitStack() as ctx:
        def sb(name, shape, dt=F32):
            return ctx.enter_context(nc.sbuf_tensor(name, shape, dt))

        def psum(name, shape, dt=F32):
            return ctx.enter_context(nc.psum_tensor(name, shape, dt))

        def sem(name):
            return ctx.enter_context(nc.semaphore(name))

        B_rows = nc.dram_tensor("B_rows", (NT * P, D), F32, kind="Internal").ap()
        run_rows = nc.dram_tensor("run_rows", (P * STEPS, 2 * D), F32, kind="Internal").ap()

        ident = sb("ident", [P, P])
        prefix_u = sb("prefix_u", [P, P])
        ones = sb("ones", [P, P])
        zeros_b = sb("zeros_b", [P, P], BF16)
        iota_i = sb("iota_i", [P, P], I32)
        iota_b = sb("iota_b", [P, P], BF16)
        part_i = sb("part_i", [P, 1], I32)
        part_f = sb("part_f", [P, 1])
        w0 = sb("w0", [P, 2 * D])
        w0T = sb("w0T", [P, 2 * D])
        w1 = sb("w1", [P, 3, D])
        w2 = sb("w2", [P, D])
        w3 = sb("w3", [P, D])
        b0_rows = sb("b0_rows", [P, D])
        b3_f = sb("b3_f", [P, 4 * D])
        b3_part = sb("b3_part", [P, 4 * D], BF16)
        b3_rows = sb("b3_rows", [P, 4 * D], BF16)
        ones_b = sb("ones_b", [P, P], BF16)
        b1_col = sb("b1_col", [P, 1])
        b2_col = sb("b2_col", [P, 1])
        eps_col = sb("eps_col", [P, 1])
        u_col = sb("u_col", [P, 1])
        c1_col = sb("c1_col", [P, 1])

        src_t = sb("src_t", [P, STEPS], I32)
        dst_t = sb("dst_t", [P, STEPS], I32)
        tmp_i = sb("tmp_i", [P, STEPS], I32)
        dst_f = sb("dst_f", [P, STEPS])
        keep = sb("keep", [P, STEPS])
        drop = sb("drop", [P, STEPS])
        lo_b = sb("lo_b", [P, STEPS], BF16)
        hi_b = sb("hi_b", [P, STEPS], BF16)
        prev_i = sb("prev_i", [P, 1], I32)
        prev_f = sb("prev_f", [P, 1])
        first_n = sb("first_n", [P, 1])
        fix_f = sb("fix_f", [P, 1])
        fix_i = sb("fix_i", [P, 1], I32)
        cont = sb("cont", [P, 1])
        cont_neg = sb("cont_neg", [P, 1])
        through = sb("through", [P, 1])
        diag = sb("diag", [P, P])
        thr_row = sb("thr_row", [P, 2, P])
        carryT = sb("carryT", [P, 2, P])
        runT = sb("runT", [P, 2, P + 1])
        fix = sb("fix", [P, 2 * D])

        X = sb("X", [P, NT, D])
        AB = sb("AB", [P, NT, 2 * D])
        A = AB[:, :, D:2 * D]
        stats = sb("stats", [P, NT, 6])
        mv = sb("mv", [P, NT, 2])
        std = sb("std", [P, NT])
        rstd = sb("rstd", [P, NT])
        nmr = sb("nmr", [P, NT])
        H = sb("H", [P, GROUP, D])
        hT = sb("hT", [P, GROUP, P])
        count = sb("count", [P, NT])
        has = sb("has", [P, NT])
        nothas = sb("nothas", [P, NT])
        tot = sb("tot", [P, NT])
        totscan = sb("totscan", [P, NT])
        end_f = sb("end_f", [P, NT])
        end_i = sb("end_i", [P, NT], I32)

        ring = sb("ring", [P, SLOTS * CHUNK * 4 * D])
        n_run = SLOTS * CHUNK * 2 * D
        n_one = SLOTS * CHUNK * D
        run = ring[:, 0:n_run].rearrange("p (s j d) -> p s j d", s=SLOTS, j=CHUNK)
        gat = ring[:, n_run:n_run + n_one].rearrange("p (s j d) -> p s j d", s=SLOTS, j=CHUNK)
        att = ring[:, n_run + n_one:n_run + 2 * n_one].rearrange("p (s j d) -> p s j d", s=SLOTS, j=CHUNK)
        ends = ring[:, 0:NT * 2 * D].rearrange("p (t d) -> p t d", t=NT)
        SM, a1, a2, ost = (
            ring[:, (NT * 2 + GROUP * m) * D:(NT * 2 + GROUP * (m + 1)) * D].rearrange("p (j d) -> p j d", j=GROUP)
            for m in range(4))
        idx = sb("idx", [P, SLOTS, CHUNK], I32)
        oh_lo = sb("oh_lo", [P, SLOTS, CHUNK, P], BF16)
        oh_hi = sb("oh_hi", [P, SLOTS, CHUNK, NT], BF16)
        z = sb("z", [P, GROUP, D])
        smT = sb("smT", [P, GROUP, P])

        pT = psum("pT", [P, 2, 512])
        pM = psum("pM", [P, 4, 512])
        pH = psum("pH", [P, 512])
        pO = psum("pO", [P, 512])

        x_in = [sem(f"x_in{g}") for g in range(NG)]
        dst_in = sem("dst_in")
        src_in = sem("src_in")
        w_in = sem("w_in")
        pad_set = sem("pad_set")
        const_set = sem("const_set")
        pool_own = sem("pool_own")
        w0_ready = sem("w0_ready")
        w0_turned = sem("w0_turned")
        dve_own = sem("dve_own")
        var1_ready = sem("var1_ready")
        std1_ready = sem("std1_ready")
        stat_ready = sem("stat_ready")
        stat_own = sem("stat_own")
        c1_ready = sem("c1_ready")
        h_ready = [sem(f"h_ready{h}") for h in range(2)]
        t_ready = [sem(f"t_ready{h}") for h in range(2)]
        hT_ready = [sem(f"hT_ready{h}") for h in range(2)]
        ab_ready = [sem(f"ab_ready{h}") for h in range(2)]
        ab_taken = [sem(f"ab_taken{h}") for h in range(2)]
        b_out = [sem(f"b_out{h}") for h in range(2)]
        init_set = sem("init_set")
        idx_ready = [sem(f"idx_ready{s}") for s in range(SLOTS)]
        gathered = [sem(f"gathered{s}") for s in range(SLOTS)]
        attr_in = [sem(f"attr_in{s}") for s in range(SLOTS)]
        rows_out = [sem(f"rows_out{s}") for s in range(SLOTS)]
        max_steps = sem("max_steps")
        sum_steps = sem("sum_steps")
        max_done = [sem(f"max_done{s}") for s in range(SLOTS)]
        sum_done = [sem(f"sum_done{s}") for s in range(SLOTS)]
        onehots = [sem(f"onehots{s}") for s in range(SLOTS)]
        counted = [sem(f"counted{s}") for s in range(SLOTS)]
        hist_done = sem("hist_done")
        count_ready = sem("count_ready")
        prefix_ready = sem("prefix_ready")
        end_ready = sem("end_ready")
        diag_ready = sem("diag_ready")
        thr_ready = sem("thr_ready")
        carry_turned = sem("carry_turned")
        run_ready = sem("run_ready")
        run_turned = sem("run_turned")
        fix_in = sem("fix_in")
        fix_ready = sem("fix_ready")
        fix_out = sem("fix_out")
        end_in = [sem(f"end_in{h}") for h in range(2)]
        var_ready = [sem(f"var_ready{h}") for h in range(2)]
        std_ready = sem("std_ready")
        x1_ready = [sem(f"x1_ready{h}") for h in range(2)]
        sm_ready = [sem(f"sm_ready{h}") for h in range(2)]
        h2_ready = [sem(f"h2_ready{h}") for h in range(2)]
        st_ready = [sem(f"st_ready{h}") for h in range(2)]
        ht_ready = [sem(f"ht_ready{h}") for h in range(2)]
        smT_ready = [sem(f"smT_ready{h}") for h in range(2)]
        h2T_ready = [sem(f"h2T_ready{h}") for h in range(2)]
        l1_ready = [sem(f"l1_ready{h}") for h in range(2)]
        a1_ready = [sem(f"a1_ready{h}") for h in range(2)]
        l2_ready = sem("l2_ready")
        a2_ready = sem("a2_ready")
        l3_ready = sem("l3_ready")
        o_ready = sem("o_ready")
        o_out = [sem(f"o_out{h}") for h in range(2)]

        x_tiles = x[0:FULL_T * P, :].rearrange("(t p) d -> p t d", p=P)
        out_tiles = out[0:FULL_T * P, :].rearrange("(t p) d -> p t d", p=P)
        B_tiles = B_rows.rearrange("(t p) d -> p t d", p=P)
        run_view = run_rows.rearrange("(p k) d -> p k d", p=P)
        LASTP = P - 1
        attr_view = attr[0:LASTP * STEPS, :].rearrange("(p k) d -> p k d", k=STEPS)
        attr_last = attr[LASTP * STEPS:E, :].rearrange("(a k) d -> a k d", a=1)
        MAINP = 112

        def load_edge_ints(eng, table, vec, signal):
            view = vec[0:LASTP * STEPS].rearrange("(p k) -> p k", k=STEPS)
            eng.dma_start(table[0:MAINP, :], view[0:MAINP, :]).then_inc(signal, 16)
            eng.dma_start(table[MAINP:LASTP, :], view[MAINP:LASTP, :]).then_inc(signal, 16)
            eng.dma_start(table[LASTP:P, 0:LAST],
                          vec[LASTP * STEPS:E].rearrange("(a k) -> a k", a=1)).then_inc(signal, 16)

        def tiles(ap, g, h):
            first, n = HALVES[h]
            return ap[:, bass.ds(g * GROUP + first, n), :]

        def ab_rows(h):
            n = HALVES[h][1]
            return pM[:, 2 * h:2 * h + 2, :].rearrange("p a b -> p (a b)")[:, 0:n * 2 * D].rearrange(
                "p (j d) -> p j d", j=n)

        block = ctx.enter_context(nc.Block())

        @block.sync
        def _(sp):
            for g in range(NG - 1):
                sp.dma_start(X[:, g * GROUP:(g + 1) * GROUP, :],
                             x_tiles[:, g * GROUP:(g + 1) * GROUP, :]).then_inc(x_in[g], 16)
            sp.wait_ge(pad_set, 5)
            sp.dma_start(X[:, (NG - 1) * GROUP:FULL_T, :], x_tiles[:, (NG - 1) * GROUP:FULL_T, :]
                         ).then_inc(x_in[NG - 1], 16)
            sp.dma_start(X[0:TAIL_N, FULL_T, :], x[FULL_T * P:N, :]).then_inc(x_in[NG - 1], 16)
            load_edge_ints(sp, dst_t, dst, dst_in)
            with nc.allow_non_contiguous_dma(reason="one value per partition"):
                sp.dma_start(prev_i[1:P, :],
                             dst[0:LASTP * STEPS].rearrange("(p k) -> p k", k=STEPS)[:, STEPS - 1:STEPS]
                             ).then_inc(dst_in, 16)

            for g in peeled(sp, NG):
                for h in range(2):
                    sp.wait_ge(ab_taken[h], g + 1)
                    sp.dma_start(tiles(B_tiles, g, h), tiles(AB, g, h)[:, :, 0:D]).then_inc(b_out[h], 16)

            def load_attr(i, s, last_row, n_last):
                k0 = i * (SLOTS * CHUNK) + s * CHUNK
                if later(i):
                    sp.wait_ge(sum_done[s], i)
                sp.dma_start(att[0:MAINP, s], attr_view[0:MAINP, bass.ds(k0, CHUNK), :]).then_inc(attr_in[s], 16)
                sp.dma_start(att[MAINP:LASTP, s], attr_view[MAINP:LASTP, bass.ds(k0, CHUNK), :]
                             ).then_inc(attr_in[s], 16)
                sp.dma_start(att[LASTP:P, s, 0:n_last], attr_last[:, bass.ds(last_row, n_last), :]
                             ).then_inc(attr_in[s], 16)

            whole = LAST // (SLOTS * CHUNK)
            for i in peeled(sp, whole):
                for s in range(SLOTS):
                    load_attr(i, s, i * (SLOTS * CHUNK) + s * CHUNK, CHUNK)
            for s in range(SLOTS):
                k0 = whole * SLOTS * CHUNK + s * CHUNK
                n_last = max(0, min(CHUNK, LAST - k0))
                load_attr(whole, s, k0 if n_last else 0, n_last or 1)
            with sp.Fori(whole + 1, LOOPS) as i:
                for s in range(SLOTS):
                    load_attr(i, s, 0, 1)

            for g in peeled(sp, NG - 1):
                for h, (first, n) in enumerate(HALVES):
                    sp.wait_ge(o_ready, g * 2 + h + 1)
                    sp.dma_start(tiles(out_tiles, g, h), ost[:, first:first + n, :]).then_inc(o_out[h], 16)
            g = NG - 1
            for h, (first, n) in enumerate(HALVES):
                sp.wait_ge(o_ready, g * 2 + h + 1)
                lo = g * GROUP + first
                n_full = min(n, FULL_T - lo)
                sp.dma_start(out_tiles[:, lo:lo + n_full, :], ost[:, first:first + n_full, :]).then_inc(o_out[h], 16)
            sp.dma_start(out[FULL_T * P:N, :], ost[0:TAIL_N, GROUP - 1, :]).then_inc(o_out[1], 16)
            sp.wait_ge(o_out[0], 16 * NG)
            sp.wait_ge(o_out[1], 16 * (NG + 1))

        @block.gpsimd
        def _(pool):
            pool.memset(ones[:], 1.0).then_inc(const_set, 1)
            pool.iota(iota_i[:], [[1, P]], base=0, channel_multiplier=0).then_inc(const_set, 1)
            pool.iota(part_i[:], [[0, 1]], base=0, channel_multiplier=STEPS).then_inc(const_set, 1)
            pool.wait_ge(const_set, 3)
            pool.affine_select(out=ident[:], in_=ones[:], compare_op=ALU.is_equal, fill=0.0, base=0,
                               pattern=[[-1, P]], channel_multiplier=1).then_inc(const_set, 1)
            pool.affine_select(out=prefix_u[:], in_=ones[:], compare_op=ALU.is_ge, fill=0.0, base=0,
                               pattern=[[1, P]], channel_multiplier=-1).then_inc(const_set, 1)

            w_loads = [
                (w0[:], W0), (w1[:], W1.rearrange("(c k) m -> k c m", k=P)), (w2[:], W2), (w3[:], W3),
                (b1_col[:], b1.rearrange("(k a) -> k a", a=1)), (b2_col[:], b2.rearrange("(k a) -> k a", a=1)),
                (u_col[:], u[0:1, :].rearrange("a k -> k a")),
                (b0_rows[:], b0.rearrange("(a k) -> a k", a=1).to_broadcast([P, D])),
                *((b3_f[32 * m:32 * m + 1, :].rearrange("a (r k) -> a r k", r=4),
                   b3.rearrange("(a r k) -> a r k", a=1, r=1).to_broadcast([1, 4, D])) for m in range(3)),
            ]
            pool.wait_ge(pad_set, 5)
            with nc.allow_non_contiguous_dma(reason="columns of 128 values"):
                for to, what in w_loads:
                    pool.dma_start(to, what).then_inc(w_in, 16)
            pool.wait_ge(pad_set, 5)
            load_edge_ints(pool, src_t, src, src_in)

            for h in range(2):
                pool.wait_ge(b_out[h], 16 * NG)

            for i in peeled(pool, LOOPS):
                for s in range(SLOTS):
                    pool.wait_ge(idx_ready[s], i + 1)
                    if later(i):
                        pool.wait_ge(max_done[s], i)
                    pool.nop(nofuse=True)
                    for j in range(CHUNK):
                        pool.indirect_dma_start(
                            gat[:, s, j, :], None, B_rows,
                            bass.IndirectOffsetOnAxis(ap=idx[:, s, j:j + 1], axis=0)).then_inc(gathered[s], 16)

            pool.wait_ge(fix_ready, 1)
            for s in range(SLOTS):
                pool.wait_ge(rows_out[s], 16 * LOOPS)
            pool.indirect_dma_start(fix[:], None, run_rows,
                                    bass.IndirectOffsetOnAxis(ap=fix_i[:], axis=0)).then_inc(fix_in, 16)
            pool.wait_ge(fix_ready, 3)
            pool.indirect_dma_start(run_rows, bass.IndirectOffsetOnAxis(ap=fix_i[:], axis=0),
                                    fix[:], None).then_inc(fix_out, 16)

            pool.wait_ge(end_ready, 1)
            pool.wait_ge(fix_out, 16)
            pool.wait_ge(run_turned, 1)
            for g in range(NG):
                for h, (first, n) in enumerate(HALVES):
                    if later(g):
                        pool.wait_ge(end_in[h], 16 * n * g)
                    for t in range(g * GROUP + first, g * GROUP + first + n):
                        pool.indirect_dma_start(
                            ends[:, t, :], None, run_rows,
                            bass.IndirectOffsetOnAxis(ap=end_i[:, t:t + 1], axis=0)).then_inc(end_in[h], 16)

        @block.scalar
        def _(act):
            def deviation(g):
                ts = bass.ds(g * GROUP, GROUP)
                act.wait_ge(var1_ready, g + 1)
                act.activation(std[:, ts], mv[:, ts, 1], ACT.Sqrt, bias=eps_col[:]).then_inc(std1_ready, 1)

            def take_products(g):
                for h in range(2):
                    act.wait_ge(ab_ready[h], g + 1)
                    act.activation(tiles(AB, g, h), ab_rows(h), ACT.Copy).then_inc(ab_taken[h], 1)

            def normalize(g):
                act.wait_ge(stat_ready, g + 1)
                for h, (first, n) in enumerate(HALVES):
                    if later(g):
                        act.wait_ge(t_ready[h], g)
                    for j in range(first, first + n):
                        t = g * GROUP + j
                        ins = act.activation(H[:, j:j + 1, :], X[:, bass.ds(t, 1), :], ACT.Relu,
                                             bias=nmr[:, bass.ds(t, 1)], scale=rstd[:, bass.ds(t, 1)])
                    ins.then_inc(h_ready[h], 1)

            deviation(0)
            normalize(0)
            deviation(1)
            with act.Fori(1, NG - 1) as g:
                normalize(g)
                deviation(g + 1)
                take_products(g - 1)
            normalize(NG - 1)
            take_products(NG - 2)
            take_products(NG - 1)

            act.wait_ge(src_in, 48)
            for s in range(SLOTS):
                act.activation(idx[:, s, :], src_t[:, s * CHUNK:(s + 1) * CHUNK], ACT.Copy).then_inc(idx_ready[s], 1)

            def store_rows(i, s):
                act.wait_ge(max_done[s], i + 1)
                act.wait_ge(sum_done[s], i + 1)
                act.dma_start(run_view[:, bass.ds(i * (SLOTS * CHUNK) + s * CHUNK, CHUNK), :],
                              run[:, s]).then_inc(rows_out[s], 16)

            for i in peeled(act, LOOPS - 1):
                for s in range(SLOTS):
                    store_rows(i, s)
                    act.wait_ge(gathered[s], i * (16 * CHUNK) + 16 * CHUNK)
                    act.activation(idx[:, s, :],
                                   src_t[:, bass.ds(i * (SLOTS * CHUNK) + (SLOTS + s) * CHUNK, CHUNK)],
                                   ACT.Copy).then_inc(idx_ready[s], 1)
            for s in range(SLOTS):
                store_rows(LOOPS - 1, s)

            act.wait_ge(end_ready, 1)
            act.wait_ge(c1_ready, 1)

            def take_sums_turned(g, h):
                first, n = HALVES[h]
                act.wait_ge(st_ready[h], g + 1)
                if later(g):
                    act.wait_ge(l1_ready[h], g)
                act.activation(smT[:, first:first + n, :], pM[:, h, 0:n * P].rearrange("p (j q) -> p j q", j=n),
                               ACT.Copy).then_inc(smT_ready[h], 1)

            def mask_sums(g, h):
                first, n = HALVES[h]
                act.wait_ge(end_in[h], g * (16 * n) + 16 * n)
                if later(g):
                    act.wait_ge(st_ready[h], g)
                for j in range(first, first + n):
                    t = g * GROUP + j
                    ins = act.activation(SM[:, j:j + 1, :], ends[:, bass.ds(t, 1), D:2 * D], ACT.Copy,
                                         scale=has[:, bass.ds(t, 1)])
                ins.then_inc(sm_ready[h], 1)

            def normalize2(g, h):
                first, n = HALVES[h]
                act.wait_ge(x1_ready[h], g + 1)
                if later(g):
                    act.wait_ge(ht_ready[h], g)
                for j in range(first, first + n):
                    ins = act.activation(H[:, j:j + 1, :], X[:, bass.ds(g * GROUP + j, 1), :], ACT.Relu,
                                         bias=nmr[:, j:j + 1], scale=rstd[:, j:j + 1])
                ins.then_inc(h2_ready[h], 1)

            def deviation2(g, h):
                first, n = HALVES[h]
                act.wait_ge(var_ready[h], g + 1)
                act.activation(std[:, first:first + n], mv[:, first:first + n, 1], ACT.Sqrt, bias=eps_col[:]
                               ).then_inc(std_ready, 1)

            def layer1_relu(g, h):
                first, n = HALVES[h]
                act.wait_ge(l1_ready[h], g + 1)
                if later(g):
                    act.wait_ge(l2_ready, g * 2 + h - 1)
                act.activation(a1[:, first:first + n, :], pM[:, 2 + h, 0:n * P].rearrange("p (j q) -> p j q", j=n),
                               ACT.Relu, bias=c1_col[:]).then_inc(a1_ready[h], 1)

            def act_tick(g, h):
                for stage, ahead in ((take_sums_turned, 0), (mask_sums, 1), (normalize2, 1), (layer1_relu, 0),
                                     (deviation2, 2)):
                    at = unit(g, h, ahead, NG)
                    if at:
                        stage(*at)

            pipeline(act, NG, act_tick, 2, 2)

        @block.tensor
        def _(pe):
            pe.wait_ge(const_set, 5)
            pe.wait_ge(w_in, 16 * 11)
            pe.transpose(pO[:, 0:P], w0[:, 0:D], ident[:])
            pe.transpose(pO[:, P:2 * P], w0[:, D:2 * D], ident[:])
            pe.matmul(pO[:, 256:257], w1[:, 2, :], u_col[:], start=True, stop=True).then_inc(w0_turned, 1)
            pe.wait_ge(init_set, 1)
            pe.matmul(pH[:, 0:NT], zeros_b[:], zeros_b[:, 0:NT], start=True, stop=False, skip_group_check=True)

            pe.wait_ge(w0_ready, 2)
            for g in peeled(pe, NG):
                for h, (first, n) in enumerate(HALVES):
                    pe.wait_ge(h_ready[h], g + 1)
                    if later(g):
                        pe.wait_ge(hT_ready[h], g)
                    for j in range(n):
                        mm = pe.transpose(pT[:, h, j * P:(j + 1) * P], H[:, first + j, :], ident[:])
                    mm.then_inc(t_ready[h], 1)
                for h, (first, n) in enumerate(HALVES):
                    pe.wait_ge(hT_ready[h], g + 1)
                    if later(g):
                        pe.wait_ge(ab_taken[h], g)
                    for j in range(n):
                        mm = pe.matmul(ab_rows(h)[:, j, :], hT[:, first + j, :], w0T[:], start=True, stop=True)
                    mm.then_inc(ab_ready[h], 1)

            for i in peeled(pe, LOOPS):
                for s in range(SLOTS):
                    pe.wait_ge(onehots[s], i * 2 + 2)
                    for j in range(CHUNK):
                        mm = pe.matmul(pH[:, 0:NT], oh_lo[:, s, j, :], oh_hi[:, s, j, :], start=False, stop=False,
                                       skip_group_check=True)
                    mm.then_inc(counted[s], 1)
            pe.matmul(pH[:, 0:NT], zeros_b[:], zeros_b[:, 0:NT], start=False, stop=True,
                      skip_group_check=True).then_inc(hist_done, 1)

            pe.wait_ge(diag_ready, 1)
            pe.matmul(pT[:, 1, 0:P], ones[:], diag[:], start=True, stop=True).then_inc(thr_ready, 1)
            pe.wait_ge(max_done[SLOTS - 1], LOOPS)
            pe.wait_ge(sum_done[SLOTS - 1], LOOPS)
            pe.transpose(pT[:, 0, 0:P], run[:, SLOTS - 1, CHUNK - 1, 0:D], ident[:])
            pe.transpose(pT[:, 0, P:2 * P], run[:, SLOTS - 1, CHUNK - 1, D:2 * D], ident[:]).then_inc(carry_turned, 1)
            pe.wait_ge(run_ready, 2)
            pe.transpose(pM[:, 0, 0:P], runT[:, 0, 0:P], ident[:])
            pe.transpose(pM[:, 0, P:2 * P], runT[:, 1, 0:P], ident[:]).then_inc(run_turned, 1)
            pe.wait_ge(count_ready, 1)
            pe.matmul(pO[:, 0:NT], prefix_u[:], count[:], start=True, stop=True)
            pe.matmul(pO[:, NT:2 * NT], ones[:], count[:], start=True, stop=True).then_inc(prefix_ready, 1)
            pe.wait_ge(fix_ready, 3)

            def turn(g, h):
                first, n = HALVES[h]
                pe.wait_ge(sm_ready[h], g + 1)
                if later(g):
                    pe.wait_ge(smT_ready[h], g)
                for j in range(n):
                    mm = pe.transpose(pM[:, h, j * P:(j + 1) * P], SM[:, first + j, :], ident[:])
                mm.then_inc(st_ready[h], 1)
                pe.wait_ge(h2_ready[h], g + 1)
                if later(g):
                    pe.wait_ge(h2T_ready[h], g)
                for j in range(n):
                    mm = pe.transpose(pT[:, h, j * P:(j + 1) * P], H[:, first + j, :], ident[:])
                mm.then_inc(ht_ready[h], 1)

            def layer1(g, h):
                first, n = HALVES[h]
                pe.wait_ge(smT_ready[h], g + 1)
                pe.wait_ge(h2T_ready[h], g + 1)
                if later(g):
                    pe.wait_ge(a1_ready[h], g)
                o = pM[:, 2 + h, 0:n * P].rearrange("p (j q) -> p j q", j=n)
                pe.matmul(o, w1[:, 0, :], hT[:, first:first + n, :], start=True, stop=False)
                pe.matmul(o, w1[:, 1, :], smT[:, first:first + n, :], start=False, stop=True
                          ).then_inc(l1_ready[h], 1)

            def layer2(g, h):
                first, n = HALVES[h]
                pe.wait_ge(a1_ready[h], g + 1)
                if later(g) or h:
                    pe.wait_ge(a2_ready, g * 2 + h)
                pe.matmul(pH[:, 0:n * P].rearrange("p (j q) -> p j q", j=n), w2[:], a1[:, first:first + n, :],
                          start=True, stop=True).then_inc(l2_ready, 1)

            def layer3(g, h):
                first, n = HALVES[h]
                if later(g) or h:
                    pe.wait_ge(o_ready, g * 2 + h)
                pe.matmul(pO[:, 0:n * P], ones_b[:], b3_rows[:, 0:n * P], start=True, stop=False,
                          skip_group_check=True)
                pe.wait_ge(a2_ready, g * 2 + h + 1)
                for j in range(n):
                    mm = pe.matmul(pO[:, j * P:(j + 1) * P], a2[:, first + j, :], w3[:], start=False,
                                   stop=(j == n - 1), skip_group_check=True)
                mm.then_inc(l3_ready, 1)

            def pe_tick(g, h):
                for stage, ahead in ((turn, 0), (layer2, -1), (layer1, 0), (layer3, -1)):
                    at = unit(g, h, ahead, NG)
                    if at:
                        stage(*at)

            pipeline(pe, NG, pe_tick, 2, 2)

        @block.vector
        def _(dve):
            dve.memset(dst_t[96:P, LAST:STEPS], PAD_DST).then_inc(pad_set, 1)
            dve.memset(src_t[96:P, LAST:STEPS], 0).then_inc(pad_set, 1)
            dve.memset(X[96:P, FULL_T, :], 0.0).then_inc(pad_set, 1)
            dve.memset(prev_i[:], -1).then_inc(pad_set, 1)
            dve.memset(b3_f[:], 0.0).then_inc(pad_set, 1)
            dve.memset(eps_col[:], EPS).then_inc(dve_own, 1)
            dve.memset(zeros_b[:], 0.0).then_inc(init_set, 1)
            dve.memset(run[:, SLOTS - 1, CHUNK - 1, 0:D], -BIG).then_inc(dve_own, 1)
            dve.memset(run[:, SLOTS - 1, CHUNK - 1, D:2 * D], 0.0).then_inc(dve_own, 1)
            dve.memset(runT[:, :, 0:1], 0.0).then_inc(dve_own, 1)
            dve.wait_ge(const_set, 5)
            dve.tensor_copy(iota_b[:], iota_i[:]).then_inc(dve_own, 1)
            dve.tensor_copy(part_f[:], part_i[:]).then_inc(dve_own, 1)

            def weights():
                dve.wait_ge(w0_turned, 1)
                dve.tensor_copy(w0T[:, 0:D], pO[:, P:2 * P]).then_inc(w0_ready, 1)
                dve.wait_ge(w0_ready, 1)
                dve.tensor_tensor(w0T[:, D:2 * D], pO[:, 0:P], w0T[:, 0:D], ALU.subtract).then_inc(w0_ready, 1)
                dve.tensor_tensor(c1_col[:], pO[:, 256:257], b1_col[:], ALU.add).then_inc(c1_ready, 1)

            def statistics(g):
                dve.wait_ge(x_in[g], 32 if g == NG - 1 else 16)
                for t in range(g * GROUP, (g + 1) * GROUP):
                    ins = dve.bn_stats(stats[:, t, :], X[:, t, :])
                ins.then_inc(stat_own, 1)
                dve.wait_ge(stat_own, 2 * g + 1)
                for t in range(g * GROUP, (g + 1) * GROUP):
                    ins = dve.bn_aggr(mv[:, t, :], stats[:, t, :])
                ins.then_inc(var1_ready, 1)

            def scale_and_shift(g):
                ts = slice(g * GROUP, (g + 1) * GROUP)
                dve.wait_ge(std1_ready, g + 1)
                dve.reciprocal(rstd[:, ts], std[:, ts]).then_inc(stat_own, 1)
                dve.wait_ge(stat_own, 2 * g + 2)
                dve.scalar_tensor_tensor(out=nmr[:, ts], in0=mv[:, ts, 0], scalar=-1.0, in1=rstd[:, ts],
                                         op0=ALU.mult, op1=ALU.mult).then_inc(stat_ready, 1)

            statistics(0)
            scale_and_shift(0)
            for g in range(NG):
                if g + 1 < NG:
                    statistics(g + 1)
                if g == 0:
                    weights()
                for h, (first, n) in enumerate(HALVES):
                    dve.wait_ge(t_ready[h], g + 1)
                    if later(g):
                        dve.wait_ge(ab_ready[h], g)
                    dve.tensor_copy(hT[:, first:first + n, :], pT[:, h, 0:n * P].rearrange("p (j q) -> p j q", j=n)
                                    ).then_inc(hT_ready[h], 1)
                if g + 1 < NG:
                    scale_and_shift(g + 1)
            own = 6

            dve.wait_ge(dst_in, 64)
            dve.tensor_copy(dst_f[:], dst_t[:]).then_inc(dve_own, 1)
            dve.tensor_copy(prev_f[:], prev_i[:]).then_inc(dve_own, 1)
            dve.tensor_scalar(tmp_i[:], dst_t[:], 7, None, ALU.logical_shift_right).then_inc(dve_own, 1)
            dve.wait_ge(dve_own, own + 3)
            dve.tensor_copy(hi_b[:], tmp_i[:]).then_inc(dve_own, 1)
            dve.tensor_scalar(drop[:], dst_f[:], dst_f[:, 0:1], None, ALU.is_equal).then_inc(dve_own, 1)
            dve.tensor_scalar(cont[:], prev_f[:], dst_f[:, 0:1], None, ALU.is_equal).then_inc(dve_own, 1)
            dve.wait_ge(dve_own, own + 6)
            dve.tensor_scalar(tmp_i[:], dst_t[:], P - 1, None, ALU.bitwise_and).then_inc(dve_own, 1)
            dve.tensor_reduce(first_n[:], drop[:], mybir.AxisListType.X, ALU.add).then_inc(dve_own, 1)
            dve.memset(keep[:, 0:1], 0.0).then_inc(dve_own, 1)
            dve.tensor_tensor(keep[:, 1:STEPS], dst_f[:, 1:STEPS], dst_f[:, 0:STEPS - 1], ALU.is_equal
                              ).then_inc(dve_own, 1)
            dve.wait_ge(dve_own, own + 10)
            dve.tensor_copy(lo_b[:], tmp_i[:]).then_inc(dve_own, 1)
            dve.tensor_scalar(drop[:], keep[:], 1.0, BIG, ALU.subtract, ALU.mult).then_inc(dve_own, 1)
            dve.scalar_tensor_tensor(out=fix_f[:], in0=first_n[:], scalar=-1.0, in1=part_f[:], op0=ALU.add,
                                     op1=ALU.add).then_inc(dve_own, 1)
            dve.tensor_scalar(through[:], first_n[:], float(STEPS), cont[:, 0:1], ALU.is_equal, ALU.mult
                              ).then_inc(dve_own, 1)
            dve.tensor_scalar(cont_neg[:], cont[:], 1.0, BIG, ALU.subtract, ALU.mult).then_inc(dve_own, 1)
            dve.wait_ge(dve_own, own + 15)
            dve.tensor_copy(fix_i[:], fix_f[:]).then_inc(fix_ready, 1)
            dve.tensor_scalar(diag[:], ident[:], through[:, 0:1], None, ALU.mult).then_inc(diag_ready, 1)
            own += 15
            dve.wait_ge(w_in, 16 * 11)
            dve.memset(b3_rows[:], 0.0).then_inc(dve_own, 1)
            dve.memset(ones_b[:], 1.0).then_inc(dve_own, 1)
            own += 2
            for m in range(3):
                dve.tensor_copy(b3_part[:], b3_f[:]).then_inc(dve_own, 1)
                dve.wait_ge(dve_own, own + 1)
                row = slice(32 * m, 32 * m + 1)
                dve.tensor_copy(b3_rows[row, :], b3_part[row, :]).then_inc(dve_own, 1)
                dve.tensor_tensor(b3_f[:], b3_f[:], b3_part[:], ALU.subtract).then_inc(dve_own, 1)
                dve.wait_ge(dve_own, own + 3)
                own += 3
            dve.wait_ge(ab_taken[0], NG)
            dve.wait_ge(ab_taken[1], NG)
            dve.tensor_tensor(A, A, b0_rows[:].rearrange("p (a d) -> p a d", a=1).to_broadcast([P, NT, D]),
                              ALU.add).then_inc(dve_own, 1)
            own += 1

            for i in peeled(dve, LOOPS):
                for s in range(SLOTS):
                    k0 = i * (SLOTS * CHUNK) + s * CHUNK
                    if later(i):
                        dve.wait_ge(counted[s], i)
                    dve.tensor_tensor(
                        oh_lo[:, s], iota_b[:].rearrange("p (a q) -> p a q", a=1).to_broadcast([P, CHUNK, P]),
                        lo_b[:, bass.ds(k0, CHUNK)].rearrange("p (k a) -> p k a", a=1).to_broadcast([P, CHUNK, P]),
                        ALU.is_equal).then_inc(onehots[s], 1)
                    dve.tensor_tensor(
                        oh_hi[:, s], iota_b[:, 0:NT].rearrange("p (a q) -> p a q", a=1).to_broadcast([P, CHUNK, NT]),
                        hi_b[:, bass.ds(k0, CHUNK)].rearrange("p (k a) -> p k a", a=1).to_broadcast([P, CHUNK, NT]),
                        ALU.is_equal).then_inc(onehots[s], 1)
                    dve.wait_ge(gathered[s], i * (16 * CHUNK) + 16 * CHUNK)
                    dve.wait_ge(attr_in[s], i * 48 + 48)
                    if later(i):
                        dve.wait_ge(rows_out[s], i * 16)
                    for j in range(CHUNK):
                        to = run[:, s, j]
                        was = run[:, s, j - 1] if j else run[:, (s - 1) % SLOTS, CHUNK - 1]
                        if j:
                            dve.wait_ge(max_steps, i * (SLOTS * (CHUNK - 1)) + s * (CHUNK - 1) + j)
                        else:
                            if later(i) or s:
                                dve.wait_ge(max_done[s - 1], i + 1 if s else i)
                        ins = dve.scalar_tensor_tensor(
                            out=to[:, 0:D], in0=was[:, 0:D], scalar=drop[:, bass.ds(k0 + j, 1)],
                            in1=gat[:, s, j, :], op0=ALU.add, op1=ALU.max)
                        if j < CHUNK - 1:
                            ins.then_inc(max_steps, 1)
                        else:
                            ins.then_inc(max_done[s], 1)
                        if j:
                            dve.wait_ge(sum_steps, i * (SLOTS * (CHUNK - 1)) + s * (CHUNK - 1) + j)
                        else:
                            if later(i) or s:
                                dve.wait_ge(sum_done[s - 1], i + 1 if s else i)
                        ins = dve.scalar_tensor_tensor(
                            out=to[:, D:2 * D], in0=was[:, D:2 * D], scalar=keep[:, bass.ds(k0 + j, 1)],
                            in1=att[:, s, j, :], op0=ALU.mult, op1=ALU.add)
                        if j < CHUNK - 1:
                            ins.then_inc(sum_steps, 1)
                        else:
                            ins.then_inc(sum_done[s], 1)

            dve.wait_ge(thr_ready, 1)
            dve.tensor_copy(thr_row[:, 1, :], pT[:, 1, 0:P]).then_inc(dve_own, 1)
            dve.tensor_scalar(thr_row[:, 0, :], pT[:, 1, 0:P], 1.0, BIG, ALU.subtract, ALU.mult).then_inc(dve_own, 1)
            dve.wait_ge(carry_turned, 1)
            dve.wait_ge(dve_own, own + 2)
            dve.tensor_tensor_scan(out=runT[:, 0, 1:P + 1], data0=thr_row[:, 0, :], data1=pT[:, 0, 0:P],
                                   initial=-BIG, op0=ALU.add, op1=ALU.max).then_inc(run_ready, 1)
            dve.tensor_tensor_scan(out=runT[:, 1, 1:P + 1], data0=thr_row[:, 1, :], data1=pT[:, 0, P:2 * P],
                                   initial=0.0, op0=ALU.mult, op1=ALU.add).then_inc(run_ready, 1)
            own += 2

            dve.wait_ge(hist_done, 1)
            dve.tensor_copy(count[:], pH[:, 0:NT]).then_inc(count_ready, 1)
            dve.wait_ge(prefix_ready, 1)
            dve.wait_ge(count_ready, 1)
            dve.tensor_scalar(has[:], count[:], 0.5, None, ALU.is_gt).then_inc(dve_own, 1)
            dve.tensor_copy(tot[:], pO[:, NT:2 * NT]).then_inc(dve_own, 1)
            dve.wait_ge(dve_own, own + 2)
            dve.tensor_scalar(nothas[:], has[:], 1.0, BIG, ALU.subtract, ALU.mult).then_inc(dve_own, 1)
            dve.memset(end_f[:], 0.0).then_inc(dve_own, 1)
            dve.wait_ge(dve_own, own + 4)
            dve.tensor_tensor_scan(out=totscan[:], data0=tot[:], data1=end_f[:], initial=0.0, op0=ALU.add,
                                   op1=ALU.add).then_inc(dve_own, 1)
            dve.wait_ge(dve_own, own + 5)
            dve.tensor_tensor(end_f[:], totscan[:], tot[:], ALU.subtract).then_inc(dve_own, 1)
            dve.wait_ge(dve_own, own + 6)
            dve.scalar_tensor_tensor(out=totscan[:], in0=pO[:, 0:NT], scalar=-1.0, in1=end_f[:], op0=ALU.add,
                                     op1=ALU.add).then_inc(dve_own, 1)
            dve.wait_ge(dve_own, own + 7)
            dve.tensor_scalar(end_i[:], totscan[:], 0.0, None, ALU.max).then_inc(end_ready, 1)
            own += 7

            dve.wait_ge(run_turned, 1)
            dve.wait_ge(fix_in, 16)
            dve.scalar_tensor_tensor(out=fix[:, 0:D], in0=pM[:, 0, 0:P], scalar=cont_neg[:, 0:1], in1=fix[:, 0:D],
                                     op0=ALU.add, op1=ALU.max).then_inc(fix_ready, 1)
            dve.scalar_tensor_tensor(out=fix[:, D:2 * D], in0=pM[:, 0, P:2 * P], scalar=cont[:, 0:1],
                                     in1=fix[:, D:2 * D], op0=ALU.mult, op1=ALU.add).then_inc(fix_ready, 1)

            def residual(g, h):
                first, n = HALVES[h]
                dve.wait_ge(end_in[h], g * (16 * n) + 16 * n)
                if later(g):
                    dve.wait_ge(h2_ready[h], g)
                base = own + (g * 2 + h) * 4
                for j in range(first, first + n):
                    t = bass.ds(g * GROUP + j, 1)
                    ins = dve.scalar_tensor_tensor(out=z[:, j:j + 1, :], in0=ends[:, t, 0:D],
                                                   scalar=nothas[:, t], in1=A[:, t, :], op0=ALU.add, op1=ALU.add)
                ins.then_inc(dve_own, 1)
                dve.wait_ge(dve_own, base + 1)
                dve.scalar_tensor_tensor(out=tiles(X, g, h), in0=z[:, first:first + n, :], scalar=0.0,
                                         in1=tiles(X, g, h), op0=ALU.max, op1=ALU.add).then_inc(dve_own, 1)
                dve.wait_ge(dve_own, base + 2)
                dve.nop(nofuse=True)
                for j in range(first, first + n):
                    ins = dve.bn_stats(stats[:, j, :], X[:, bass.ds(g * GROUP + j, 1), :])
                ins.then_inc(dve_own, 1)
                dve.wait_ge(dve_own, base + 3)
                dve.nop(nofuse=True)
                for j in range(first, first + n):
                    ins = dve.bn_aggr(mv[:, j, :], stats[:, j, :])
                ins.then_inc(var_ready[h], 1)

            def scale_and_shift2(g, h):
                first, n = HALVES[h]
                ts = slice(first, first + n)
                dve.wait_ge(std_ready, g * 2 + h + 1)
                dve.reciprocal(rstd[:, ts], std[:, ts]).then_inc(dve_own, 1)
                dve.wait_ge(dve_own, own + (g * 2 + h) * 4 + 4)
                dve.scalar_tensor_tensor(out=nmr[:, ts], in0=mv[:, ts, 0], scalar=-1.0, in1=rstd[:, ts],
                                         op0=ALU.mult, op1=ALU.mult).then_inc(x1_ready[h], 1)

            def take_h_turned(g, h):
                first, n = HALVES[h]
                dve.wait_ge(ht_ready[h], g + 1)
                if later(g):
                    dve.wait_ge(l1_ready[h], g)
                dve.tensor_copy(hT[:, first:first + n, :], pT[:, h, 0:n * P].rearrange("p (j q) -> p j q", j=n)
                                ).then_inc(h2T_ready[h], 1)

            def layer2_relu(g, h):
                first, n = HALVES[h]
                dve.wait_ge(l2_ready, g * 2 + h + 1)
                if later(g):
                    dve.wait_ge(l3_ready, g * 2 + h - 1)
                dve.tensor_scalar(a2[:, first:first + n, :], pH[:, 0:n * P].rearrange("p (j q) -> p j q", j=n),
                                  b2_col[:, 0:1], 0.0, ALU.add, ALU.max).then_inc(a2_ready, 1)

            def result(g, h):
                first, n = HALVES[h]
                dve.wait_ge(l3_ready, g * 2 + h + 1)
                if later(g):
                    dve.wait_ge(o_out[h], g * 16)
                dve.tensor_tensor(ost[:, first:first + n, :], pO[:, 0:n * P].rearrange("p (j q) -> p j q", j=n),
                                  tiles(X, g, h), ALU.add).then_inc(o_ready, 1)

            def dve_tick(g, h):
                for stage, ahead in ((result, -2), (take_h_turned, 0), (layer2_relu, -1), (residual, 2),
                                     (scale_and_shift2, 2)):
                    at = unit(g, h, ahead, NG)
                    if at:
                        stage(*at)

            pipeline(dve, NG, dve_tick, 2, 2)


_NAMES = ['x', 'src', 'dst', 'edge_attr_128', 'L0_gnn_W', 'L0_gnn_b', 'L1_gnn_u', 'L1_gnn_W1', 'L1_gnn_b1',
          'L1_gnn_W2', 'L1_gnn_b2', 'L1_gnn_W3', 'L1_gnn_b3']


def kernel(**inputs):
    import concourse.bacc as bacc
    from concourse.bass_utils import run_bass_kernel_spmd

    nc = bacc.Bacc("TRN2", target_bir_lowering=False, num_devices=1)
    arrays = {f"{n}_dram": np.ascontiguousarray(inputs[n]) for n in _NAMES}
    args = [nc.dram_tensor(n, a.shape, mybir.dt.from_np(a.dtype), kind="ExternalInput").ap()
            for n, a in arrays.items()]
    out = nc.dram_tensor("out_dram", tuple(inputs['x'].shape), F32, kind="ExternalOutput").ap()
    gnn_block(nc, *args, out)
    return run_bass_kernel_spmd(nc, [arrays], core_ids=[0]).results[0]["out_dram"]
```

```python
from contextlib import ExitStack

import numpy as np

import concourse.bass as bass
from concourse import mybir

ALU = mybir.AluOpType
ACT = mybir.ActivationFunctionType
F32 = mybir.dt.float32
BF16 = mybir.dt.bfloat16
I32 = mybir.dt.int32

P = 128
D = 128
BIG = 3.0e38
EPS = 1e-5
CHUNK = 8
SLOTS = 4
LAST_PIECES = [(0, 4), (4, 7), (7, 8)]


def peeled(engine, count):
    yield 0
    with engine.Fori(1, count) as i:
        yield i


def later(i):
    return not (isinstance(i, int) and i == 0)


def pipeline(engine, groups, tick, before, after):
    first = -(-after // 2)
    last = groups - -(-before // 2)
    for u in range(-before, 2 * first):
        tick(u // 2, u % 2)
    with engine.Fori(first, last) as g:
        for h in range(2):
            tick(g, h)
    for u in range(2 * last, 2 * groups + after):
        tick(u // 2, u % 2)


def unit(g, h, ahead, groups):
    g, h = g + (h + ahead) // 2, (h + ahead) % 2
    return None if isinstance(g, int) and not 0 <= g < groups else (g, h)


def gnn_block(nc, x, src, dst, attr, W0, b0, u, W1, b1, W2, b2, W3, b3, out):
    N, E = x.shape[0], attr.shape[0]
    NT = -(-N // P)
    FULL_T = N // P
    TAIL_N = N - FULL_T * P
    GROUP = 7
    NG = NT // GROUP
    HALVES = [(0, 4), (4, 3)]
    assert NT == NG * GROUP and TAIL_N > 0 and FULL_T == NT - 1
    STEPS = -(-(-(-E // P)) // (CHUNK * SLOTS)) * CHUNK * SLOTS
    LAST = E - (P - 1) * STEPS
    assert 0 < LAST < STEPS
    LOOPS = STEPS // (CHUNK * SLOTS)
    PAD_DST = 8191

    with ExitStack() as ctx:
        def sb(name, shape, dt=F32):
            return ctx.enter_context(nc.sbuf_tensor(name, shape, dt))

        def psum(name, shape, dt=F32):
            return ctx.enter_context(nc.psum_tensor(name, shape, dt))

        def sem(name):
            return ctx.enter_context(nc.semaphore(name))

        B_rows = nc.dram_tensor("B_rows", (NT * P, D), F32, kind="Internal").ap()
        NO_EDGES = P * STEPS
        run_rows = nc.dram_tensor("run_rows", (P * STEPS + 1, 2 * D), F32, kind="Internal").ap()

        ident = sb("ident", [P, P])
        prefix_u = sb("prefix_u", [P, P])
        ones = sb("ones", [P, P])
        zeros_b = sb("zeros_b", [P, P], BF16)
        iota_i = sb("iota_i", [P, P], I32)
        iota_b = sb("iota_b", [P, P], BF16)
        part_i = sb("part_i", [P, 1], I32)
        part_f = sb("part_f", [P, 1])
        w0 = sb("w0", [P, 2 * D])
        w0T = sb("w0T", [P, 2 * D])
        w1 = sb("w1", [P, 3, D])
        w2 = sb("w2", [P, D])
        w3 = sb("w3", [P, D])
        b0_rows = sb("b0_rows", [P, D])
        b3_f = sb("b3_f", [P, 4 * D])
        b3_part = sb("b3_part", [P, 4 * D], BF16)
        b3_rows = sb("b3_rows", [P, 4 * D], BF16)
        ones_b = sb("ones_b", [P, P], BF16)
        b1_col = sb("b1_col", [P, 1])
        b2_col = sb("b2_col", [P, 1])
        eps_col = sb("eps_col", [P, 1])
        u_col = sb("u_col", [P, 1])
        c1_col = sb("c1_col", [P, 1])

        src_t = sb("src_t", [P, STEPS], I32)
        dst_t = sb("dst_t", [P, STEPS], I32)
        tmp_i = sb("tmp_i", [P, STEPS], I32)
        dst_f = sb("dst_f", [P, STEPS])
        keep = sb("keep", [P, STEPS])
        drop = sb("drop", [P, STEPS])
        lo_b = sb("lo_b", [P, STEPS], BF16)
        hi_b = sb("hi_b", [P, STEPS], BF16)
        prev_i = sb("prev_i", [P, 1], I32)
        prev_f = sb("prev_f", [P, 1])
        first_n = sb("first_n", [P, 1])
        fix_f = sb("fix_f", [P, 1])
        fix_i = sb("fix_i", [P, 1], I32)
        cont = sb("cont", [P, 1])
        cont_neg = sb("cont_neg", [P, 1])
        through = sb("through", [P, 1])
        diag = sb("diag", [P, P])
        thr_row = sb("thr_row", [P, 2, P])
        runT = sb("runT", [P, 2, P + 1])
        fix = sb("fix", [P, 2 * D])
        no_edges_row = sb("no_edges_row", [1, 2 * D])

        X = sb("X", [P, NT, D])
        AB = sb("AB", [P, NT, 2 * D])
        A = AB[:, :, D:2 * D]
        HT = A
        stats = sb("stats", [P, NT, 6])
        mv = sb("mv", [P, NT, 2])
        std = sb("std", [P, NT])
        rstd = sb("rstd", [P, NT])
        nmr = sb("nmr", [P, NT])
        H = sb("H", [P, GROUP, D])
        hT = sb("hT", [P, GROUP, P])
        count = sb("count", [P, NT])
        has = sb("has", [P, NT])
        tot = sb("tot", [P, NT])
        totscan = sb("totscan", [P, NT])
        end_f = sb("end_f", [P, NT])
        end_i = sb("end_i", [P, NT], I32)

        ring = sb("ring", [P, SLOTS * CHUNK * 4 * D])
        n_run = SLOTS * CHUNK * 2 * D
        n_one = SLOTS * CHUNK * D
        run = ring[:, 0:n_run].rearrange("p (s j d) -> p s j d", s=SLOTS, j=CHUNK)
        gat = ring[:, n_run:n_run + n_one].rearrange("p (s j d) -> p s j d", s=SLOTS, j=CHUNK)
        att = ring[:, n_run + n_one:n_run + 2 * n_one].rearrange("p (s j d) -> p s j d", s=SLOTS, j=CHUNK)
        ends = ring[:, 0:NT * 2 * D].rearrange("p (t d) -> p t d", t=NT)
        a1, a2, ost = (
            ring[:, (NT * 2 + GROUP * m) * D:(NT * 2 + GROUP * (m + 1)) * D].rearrange("p (j d) -> p j d", j=GROUP)
            for m in range(3))
        idx = sb("idx", [P, SLOTS, CHUNK], I32)
        oh_lo = sb("oh_lo", [P, SLOTS, CHUNK, P], BF16)
        oh_hi = sb("oh_hi", [P, SLOTS, CHUNK, NT], BF16)
        z = sb("z", [P, GROUP, D])
        smT = sb("smT", [P, GROUP, P])

        pT = psum("pT", [P, 2, 512])
        pM = psum("pM", [P, 4, 512])
        pH = psum("pH", [P, 512])
        pO = psum("pO", [P, 512])

        x_in = [sem(f"x_in{g}") for g in range(NG)]
        dst_in = sem("dst_in")
        src_in = sem("src_in")
        w_in = sem("w_in")
        w0_in = sem("w0_in")
        pad_set = sem("pad_set")
        const_set = sem("const_set")
        w0_ready = sem("w0_ready")
        w0_turned = sem("w0_turned")
        dve_own = sem("dve_own")
        var1_ready = sem("var1_ready")
        std1_ready = sem("std1_ready")
        stat_ready = sem("stat_ready")
        stat_own = sem("stat_own")
        u_ready = sem("u_ready")
        c1_ready = sem("c1_ready")
        h_ready = [sem(f"h_ready{h}") for h in range(2)]
        t_ready = [sem(f"t_ready{h}") for h in range(2)]
        hT_ready = [sem(f"hT_ready{h}") for h in range(2)]
        b_ready = [sem(f"b_ready{h}") for h in range(2)]
        b_taken = [sem(f"b_taken{h}") for h in range(2)]
        a_ready = [sem(f"a_ready{h}") for h in range(2)]
        a_taken = [sem(f"a_taken{h}") for h in range(2)]
        b_out = [sem(f"b_out{h}") for h in range(2)]
        init_set = sem("init_set")
        idx_ready = [sem(f"idx_ready{s}") for s in range(SLOTS)]
        last_gathered = [sem(f"last_gathered{j}") for j in range(CHUNK)]
        none_set = sem("none_set")
        none_out = sem("none_out")
        gathered = [sem(f"gathered{s}") for s in range(SLOTS)]
        attr_in = [sem(f"attr_in{s}") for s in range(SLOTS)]
        rows_out = [sem(f"rows_out{s}") for s in range(SLOTS)]
        max_steps = sem("max_steps")
        sum_steps = sem("sum_steps")
        max_done = [sem(f"max_done{s}") for s in range(SLOTS)]
        sum_done = [sem(f"sum_done{s}") for s in range(SLOTS)]
        onehots = [sem(f"onehots{s}") for s in range(SLOTS)]
        counted = [sem(f"counted{s}") for s in range(SLOTS)]
        hist_done = sem("hist_done")
        count_ready = sem("count_ready")
        prefix_ready = sem("prefix_ready")
        end_ready = sem("end_ready")
        diag_ready = sem("diag_ready")
        thr_ready = sem("thr_ready")
        carry_turned = sem("carry_turned")
        run_ready = sem("run_ready")
        run_turned = sem("run_turned")
        fix_in = sem("fix_in")
        fix_ready = sem("fix_ready")
        fix_out = sem("fix_out")
        end_in = [sem(f"end_in{h}") for h in range(2)]
        var_ready = [sem(f"var_ready{h}") for h in range(2)]
        std_ready = sem("std_ready")
        rstd2_ready = sem("rstd2_ready")
        x1_ready = [sem(f"x1_ready{h}") for h in range(2)]
        h2_ready = [sem(f"h2_ready{h}") for h in range(2)]
        st_ready = [sem(f"st_ready{h}") for h in range(2)]
        ht_ready = [sem(f"ht_ready{h}") for h in range(2)]
        smT_ready = [sem(f"smT_ready{h}") for h in range(2)]
        h2T_ready = [sem(f"h2T_ready{h}") for h in range(2)]
        l1_ready = [sem(f"l1_ready{h}") for h in range(2)]
        a1_ready = [sem(f"a1_ready{h}") for h in range(2)]
        l2_ready = sem("l2_ready")
        a2_ready = sem("a2_ready")
        l3_ready = sem("l3_ready")
        o_ready = sem("o_ready")
        o_out = [sem(f"o_out{h}") for h in range(2)]

        x_tiles = x[0:FULL_T * P, :].rearrange("(t p) d -> p t d", p=P)
        out_tiles = out[0:FULL_T * P, :].rearrange("(t p) d -> p t d", p=P)
        B_tiles = B_rows.rearrange("(t p) d -> p t d", p=P)
        run_view = run_rows[0:P * STEPS, :].rearrange("(p k) d -> p k d", p=P)
        LASTP = P - 1
        attr_view = attr[0:LASTP * STEPS, :].rearrange("(p k) d -> p k d", k=STEPS)
        attr_last = attr[LASTP * STEPS:E, :].rearrange("(a k) d -> a k d", a=1)
        MAINP = 112

        def load_edge_ints(eng, table, vec, signal):
            view = vec[0:LASTP * STEPS].rearrange("(p k) -> p k", k=STEPS)
            eng.dma_start(table[0:MAINP, :], view[0:MAINP, :]).then_inc(signal, 16)
            eng.dma_start(table[MAINP:LASTP, :], view[MAINP:LASTP, :]).then_inc(signal, 16)
            eng.dma_start(table[LASTP:P, 0:LAST],
                          vec[LASTP * STEPS:E].rearrange("(a k) -> a k", a=1)).then_inc(signal, 16)

        def tiles(ap, g, h):
            first, n = HALVES[h]
            return ap[:, bass.ds(g * GROUP + first, n), :]

        def by_tile(bank, h):
            n = HALVES[h][1]
            return bank[:, 0:n * P].rearrange("p (j d) -> p j d", j=n)

        block = ctx.enter_context(nc.Block())

        @block.sync
        def _(sp):
            for g in range(NG - 1):
                sp.dma_start(X[:, g * GROUP:(g + 1) * GROUP, :],
                             x_tiles[:, g * GROUP:(g + 1) * GROUP, :]).then_inc(x_in[g], 16)
            sp.wait_ge(pad_set, 5)
            sp.dma_start(X[:, (NG - 1) * GROUP:FULL_T, :], x_tiles[:, (NG - 1) * GROUP:FULL_T, :]
                         ).then_inc(x_in[NG - 1], 16)
            sp.dma_start(X[0:TAIL_N, FULL_T, :], x[FULL_T * P:N, :]).then_inc(x_in[NG - 1], 16)
            load_edge_ints(sp, dst_t, dst, dst_in)
            with nc.allow_non_contiguous_dma(reason="one value per partition"):
                sp.dma_start(prev_i[1:P, :],
                             dst[0:LASTP * STEPS].rearrange("(p k) -> p k", k=STEPS)[:, STEPS - 1:STEPS]
                             ).then_inc(dst_in, 16)

            load_edge_ints(sp, src_t, src, src_in)
            sp.wait_ge(none_set, 2)
            sp.dma_start(run_rows[NO_EDGES:NO_EDGES + 1, :], no_edges_row[:]).then_inc(none_out, 16)
            w_loads = [
                (w1[:], W1.rearrange("(c k) m -> k c m", k=P)), (w2[:], W2), (w3[:], W3),
                (b1_col[:], b1.rearrange("(k a) -> k a", a=1)), (b2_col[:], b2.rearrange("(k a) -> k a", a=1)),
                (u_col[:], u[0:1, :].rearrange("a k -> k a")),
                (b0_rows[:], b0.rearrange("(a k) -> a k", a=1).to_broadcast([P, D])),
                *((b3_f[32 * m:32 * m + 1, :].rearrange("a (r k) -> a r k", r=4),
                   b3.rearrange("(a r k) -> a r k", a=1, r=1).to_broadcast([1, 4, D])) for m in range(3)),
            ]
            with nc.allow_non_contiguous_dma(reason="columns of 128 values"):
                for to, what in w_loads:
                    sp.dma_start(to, what).then_inc(w_in, 16)

            for g in peeled(sp, NG):
                for h in range(2):
                    sp.wait_ge(b_taken[h], g + 1)
                    sp.dma_start(tiles(B_tiles, g, h), tiles(AB, g, h)[:, :, 0:D]).then_inc(b_out[h], 16)

            def load_attr(i, s, last_row, n_last):
                k0 = i * (SLOTS * CHUNK) + s * CHUNK
                if later(i):
                    sp.wait_ge(sum_done[s], i)
                sp.dma_start(att[0:MAINP, s], attr_view[0:MAINP, bass.ds(k0, CHUNK), :]).then_inc(attr_in[s], 16)
                sp.dma_start(att[MAINP:LASTP, s], attr_view[MAINP:LASTP, bass.ds(k0, CHUNK), :]
                             ).then_inc(attr_in[s], 16)
                sp.dma_start(att[LASTP:P, s, 0:n_last], attr_last[:, bass.ds(last_row, n_last), :]
                             ).then_inc(attr_in[s], 16)

            whole = LAST // (SLOTS * CHUNK)
            for i in peeled(sp, whole):
                for s in range(SLOTS):
                    load_attr(i, s, i * (SLOTS * CHUNK) + s * CHUNK, CHUNK)
            for s in range(SLOTS):
                k0 = whole * SLOTS * CHUNK + s * CHUNK
                n_last = max(0, min(CHUNK, LAST - k0))
                load_attr(whole, s, k0 if n_last else 0, n_last or 1)
            with sp.Fori(whole + 1, LOOPS) as i:
                for s in range(SLOTS):
                    load_attr(i, s, 0, 1)

            for g in peeled(sp, NG - 1):
                for h, (first, n) in enumerate(HALVES):
                    sp.wait_ge(o_ready, g * 2 + h + 1)
                    sp.dma_start(tiles(out_tiles, g, h), ost[:, first:first + n, :]).then_inc(o_out[h], 16)
            g = NG - 1
            for h, (first, n) in enumerate(HALVES):
                sp.wait_ge(o_ready, g * 2 + h + 1)
                lo = g * GROUP + first
                n_full = min(n, FULL_T - lo)
                sp.dma_start(out_tiles[:, lo:lo + n_full, :], ost[:, first:first + n_full, :]).then_inc(o_out[h], 16)
            sp.dma_start(out[FULL_T * P:N, :], ost[0:TAIL_N, GROUP - 1, :]).then_inc(o_out[1], 16)
            sp.wait_ge(o_out[0], 16 * NG)
            sp.wait_ge(o_out[1], 16 * (NG + 1))

        @block.gpsimd
        def _(pool):
            pool.memset(ones[:], 1.0).then_inc(const_set, 1)
            pool.iota(iota_i[:], [[1, P]], base=0, channel_multiplier=0).then_inc(const_set, 1)
            pool.iota(part_i[:], [[0, 1]], base=0, channel_multiplier=STEPS).then_inc(const_set, 1)
            pool.wait_ge(const_set, 3)
            pool.affine_select(out=ident[:], in_=ones[:], compare_op=ALU.is_equal, fill=0.0, base=0,
                               pattern=[[-1, P]], channel_multiplier=1).then_inc(const_set, 1)
            pool.affine_select(out=prefix_u[:], in_=ones[:], compare_op=ALU.is_ge, fill=0.0, base=0,
                               pattern=[[1, P]], channel_multiplier=-1).then_inc(const_set, 1)

            for g in peeled(pool, NG):
                pool.wait_ge(var1_ready, g + 1)
                for h, (first, n) in enumerate(HALVES):
                    if later(g):
                        pool.wait_ge(t_ready[h], g)
                    pool.tensor_tensor(
                        H[:, first:first + n, :], tiles(X, g, h),
                        mv[:, bass.ds(g * GROUP + first, n), 0:1].to_broadcast([P, n, D]), ALU.subtract
                    ).then_inc(h_ready[h], 1)

            for h in range(2):
                pool.wait_ge(b_out[h], 16 * NG)

            def gather(i, s, signals):
                pool.wait_ge(idx_ready[s], i + 1)
                if later(i):
                    pool.wait_ge(max_done[s], i)
                pool.nop(nofuse=True)
                for j in range(CHUNK):
                    pool.indirect_dma_start(
                        gat[:, s, j, :], None, B_rows,
                        bass.IndirectOffsetOnAxis(ap=idx[:, s, j:j + 1], axis=0)).then_inc(signals[j], 16)

            for i in peeled(pool, LOOPS - 1):
                for s in range(SLOTS):
                    gather(i, s, [gathered[s]] * CHUNK)
            for s in range(SLOTS):
                gather(LOOPS - 1, s, [gathered[s]] * CHUNK if s < SLOTS - 1 else last_gathered)

            pool.wait_ge(fix_ready, 1)
            for s in range(SLOTS):
                pool.wait_ge(rows_out[s], 16 * (LOOPS if s < SLOTS - 1 else LOOPS - 1 + len(LAST_PIECES)))
            pool.indirect_dma_start(fix[:], None, run_rows,
                                    bass.IndirectOffsetOnAxis(ap=fix_i[:], axis=0)).then_inc(fix_in, 16)
            pool.wait_ge(fix_ready, 3)
            pool.indirect_dma_start(run_rows, bass.IndirectOffsetOnAxis(ap=fix_i[:], axis=0),
                                    fix[:], None).then_inc(fix_out, 16)

            pool.wait_ge(end_ready, 1)
            pool.wait_ge(none_out, 16)
            pool.wait_ge(fix_out, 16)
            pool.wait_ge(run_turned, 1)
            for g in range(NG):
                for h, (first, n) in enumerate(HALVES):
                    if later(g):
                        pool.wait_ge(end_in[h], 16 * n * g)
                    for t in range(g * GROUP + first, g * GROUP + first + n):
                        pool.indirect_dma_start(
                            ends[:, t, :], None, run_rows,
                            bass.IndirectOffsetOnAxis(ap=end_i[:, t:t + 1], axis=0)).then_inc(end_in[h], 16)

        @block.scalar
        def _(act):
            act.dma_start(w0[:], W0).then_inc(w0_in, 16)

            def deviation(g):
                ts = bass.ds(g * GROUP, GROUP)
                act.wait_ge(var1_ready, g + 1)
                act.activation(std[:, ts], mv[:, ts, 1], ACT.Sqrt, bias=eps_col[:]).then_inc(std1_ready, 1)

            def take_turned(g):
                for h in range(2):
                    act.wait_ge(t_ready[h], g + 1)
                    act.activation(tiles(HT, g, h), by_tile(pT[:, h], h), ACT.Relu).then_inc(hT_ready[h], 1)

            def take_scaled(g, h, ready, taken, columns, bank):
                first, n = HALVES[h]
                act.wait_ge(ready[h], g + 1)
                for j in range(n):
                    t = bass.ds(g * GROUP + first + j, 1)
                    ins = act.activation(AB[:, t, columns], by_tile(bank, h)[:, j:j + 1, :], ACT.Copy,
                                         scale=rstd[:, t])
                ins.then_inc(taken[h], 1)

            def take_B(g):
                act.wait_ge(stat_ready, g + 1)
                take_scaled(g, 1, b_ready, b_taken, slice(0, D), pM[:, 1])

            deviation(0)
            take_turned(0)
            deviation(1)
            with act.Fori(1, NG - 1) as g:
                take_turned(g)
                deviation(g + 1)
                take_B(g - 1)
            take_turned(NG - 1)
            take_B(NG - 2)
            take_B(NG - 1)

            act.wait_ge(src_in, 48)
            for s in range(SLOTS):
                act.activation(idx[:, s, :], src_t[:, s * CHUNK:(s + 1) * CHUNK], ACT.Copy).then_inc(idx_ready[s], 1)

            for g in peeled(act, NG):
                for h in range(2):
                    take_scaled(g, h, a_ready, a_taken, slice(D, 2 * D), pM[:, 2 + h])

            def store_rows(i, s):
                act.wait_ge(max_done[s], i + 1)
                act.wait_ge(sum_done[s], i + 1)
                act.dma_start(run_view[:, bass.ds(i * (SLOTS * CHUNK) + s * CHUNK, CHUNK), :],
                              run[:, s]).then_inc(rows_out[s], 16)

            for i in peeled(act, LOOPS - 1):
                for s in range(SLOTS):
                    store_rows(i, s)
                    act.wait_ge(gathered[s], i * (16 * CHUNK) + 16 * CHUNK)
                    act.activation(idx[:, s, :],
                                   src_t[:, bass.ds(i * (SLOTS * CHUNK) + (SLOTS + s) * CHUNK, CHUNK)],
                                   ACT.Copy).then_inc(idx_ready[s], 1)
            for s in range(SLOTS - 1):
                store_rows(LOOPS - 1, s)
            i, s = LOOPS - 1, SLOTS - 1
            for lo, hi in LAST_PIECES:
                if hi < CHUNK:
                    done = (i * SLOTS + s) * (CHUNK - 1) + hi
                    act.wait_ge(max_steps, done)
                    act.wait_ge(sum_steps, done)
                else:
                    act.wait_ge(max_done[s], i + 1)
                    act.wait_ge(sum_done[s], i + 1)
                act.dma_start(run_view[:, STEPS - CHUNK + lo:STEPS - CHUNK + hi, :],
                              run[:, s, lo:hi]).then_inc(rows_out[s], 16)

            act.wait_ge(end_ready, 1)
            act.wait_ge(c1_ready, 1)

            def take_sums_turned(g, h):
                first, n = HALVES[h]
                act.wait_ge(st_ready[h], g + 1)
                if later(g):
                    act.wait_ge(l1_ready[h], g)
                act.activation(smT[:, first:first + n, :], pM[:, h, 0:n * P].rearrange("p (j q) -> p j q", j=n),
                               ACT.Copy).then_inc(smT_ready[h], 1)

            def take_h_turned(g, h):
                if not h:
                    return
                first, n = HALVES[h]
                act.wait_ge(ht_ready[h], g + 1)
                if later(g):
                    act.wait_ge(l1_ready[h], g)
                act.activation(hT[:, first:first + n, :], by_tile(pT[:, h], h), ACT.Copy).then_inc(h2T_ready[h], 1)

            def normalize2(g, h):
                first, n = HALVES[h]
                act.wait_ge(x1_ready[h], g + 1)
                if later(g):
                    act.wait_ge(ht_ready[h], g)
                for j in range(first, first + n):
                    ins = act.activation(H[:, j:j + 1, :], X[:, bass.ds(g * GROUP + j, 1), :], ACT.Relu,
                                         bias=nmr[:, j:j + 1], scale=rstd[:, j:j + 1])
                ins.then_inc(h2_ready[h], 1)

            def deviation2(g, h):
                first, n = HALVES[h]
                act.wait_ge(var_ready[h], g + 1)
                act.activation(std[:, first:first + n], mv[:, first:first + n, 1], ACT.Sqrt, bias=eps_col[:]
                               ).then_inc(std_ready, 1)

            def layer1_relu(g, h):
                first, n = HALVES[h]
                act.wait_ge(l1_ready[h], g + 1)
                if later(g):
                    act.wait_ge(l2_ready, g * 2 + h - 1)
                act.activation(a1[:, first:first + n, :], pM[:, 2 + h, 0:n * P].rearrange("p (j q) -> p j q", j=n),
                               ACT.Relu, bias=c1_col[:]).then_inc(a1_ready[h], 1)

            def layer2_relu(g, h):
                first, n = HALVES[h]
                act.wait_ge(l2_ready, g * 2 + h + 1)
                if later(g):
                    act.wait_ge(l3_ready, g * 2 + h - 1)
                act.activation(a2[:, first:first + n, :], by_tile(pH, h), ACT.Relu, bias=b2_col[:]
                               ).then_inc(a2_ready, 1)

            def act_tick(g, h):
                for stage, ahead in ((deviation2, 1), (take_sums_turned, 0), (take_h_turned, 0), (normalize2, 1), (layer2_relu, -1),
                                     (layer1_relu, 0)):
                    at = unit(g, h, ahead, NG)
                    if at:
                        stage(*at)

            pipeline(act, NG, act_tick, 2, 2)

        @block.tensor
        def _(pe):
            pe.wait_ge(const_set, 5)
            pe.wait_ge(w0_in, 16)
            pe.transpose(pO[:, 0:P], w0[:, 0:D], ident[:])
            pe.transpose(pO[:, P:2 * P], w0[:, D:2 * D], ident[:]).then_inc(w0_turned, 1)
            pe.wait_ge(init_set, 1)
            pe.matmul(pH[:, 0:NT], zeros_b[:], zeros_b[:, 0:NT], start=True, stop=False, skip_group_check=True)

            def turn1(g):
                for h, (first, n) in enumerate(HALVES):
                    pe.wait_ge(h_ready[h], g + 1)
                    if g:
                        pe.wait_ge(hT_ready[h], g)
                    for j in range(n):
                        mm = pe.transpose(pT[:, h, j * P:(j + 1) * P], H[:, first + j, :], ident[:])
                    mm.then_inc(t_ready[h], 1)

            def product(g, h, bank, weight, ready, taken):
                first, n = HALVES[h]
                if g:
                    pe.wait_ge(taken[h], g)
                for j in range(n):
                    mm = pe.matmul(by_tile(bank, h)[:, j, :], HT[:, g * GROUP + first + j, :], weight,
                                   start=True, stop=True)
                mm.then_inc(ready[h], 1)

            pe.wait_ge(w0_ready, 2)
            turn1(0)
            for g in range(NG):
                if g + 1 < NG:
                    turn1(g + 1)
                for h in range(2):
                    pe.wait_ge(hT_ready[h], g + 1)
                    product(g, h, pM[:, h], w0T[:, 0:D], b_ready, b_taken)
            for g in range(NG):
                for h in range(2):
                    product(g, h, pM[:, 2 + h], w0T[:, D:2 * D], a_ready, a_taken)
            pe.wait_ge(w_in, 16 * 10)
            pe.matmul(pO[:, 256:257], w1[:, 2, :], u_col[:], start=True, stop=True).then_inc(u_ready, 1)

            pe.wait_ge(diag_ready, 1)
            pe.matmul(pT[:, 1, 0:P], ones[:], diag[:], start=True, stop=True).then_inc(thr_ready, 1)

            for i in peeled(pe, LOOPS):
                for s in range(SLOTS):
                    pe.wait_ge(onehots[s], i * 2 + 2)
                    for j in range(CHUNK):
                        mm = pe.matmul(pH[:, 0:NT], oh_lo[:, s, j, :], oh_hi[:, s, j, :], start=False, stop=False,
                                       skip_group_check=True)
                    mm.then_inc(counted[s], 1)
            pe.matmul(pH[:, 0:NT], zeros_b[:], zeros_b[:, 0:NT], start=False, stop=True,
                      skip_group_check=True).then_inc(hist_done, 1)

            pe.wait_ge(max_done[SLOTS - 1], LOOPS)
            pe.wait_ge(sum_done[SLOTS - 1], LOOPS)
            pe.transpose(pT[:, 0, 0:P], run[:, SLOTS - 1, CHUNK - 1, 0:D], ident[:])
            pe.transpose(pT[:, 0, P:2 * P], run[:, SLOTS - 1, CHUNK - 1, D:2 * D], ident[:]).then_inc(carry_turned, 1)
            pe.wait_ge(run_ready, 2)
            pe.transpose(pM[:, 0, 0:P], runT[:, 0, 0:P], ident[:])
            pe.transpose(pM[:, 0, P:2 * P], runT[:, 1, 0:P], ident[:]).then_inc(run_turned, 1)
            pe.wait_ge(count_ready, 1)
            pe.matmul(pO[:, 0:NT], prefix_u[:], count[:], start=True, stop=True)
            pe.matmul(pO[:, NT:2 * NT], ones[:], count[:], start=True, stop=True).then_inc(prefix_ready, 1)
            pe.wait_ge(fix_ready, 3)

            def turn(g, h):
                first, n = HALVES[h]
                pe.wait_ge(end_in[h], (g + 1) * 16 * n)
                if later(g):
                    pe.wait_ge(smT_ready[h], g)
                for j in range(n):
                    mm = pe.transpose(pM[:, h, j * P:(j + 1) * P], ends[:, g * GROUP + first + j, D:2 * D], ident[:])
                mm.then_inc(st_ready[h], 1)
                pe.wait_ge(h2_ready[h], g + 1)
                if later(g):
                    pe.wait_ge(h2T_ready[h], g)
                for j in range(n):
                    mm = pe.transpose(pT[:, h, j * P:(j + 1) * P], H[:, first + j, :], ident[:])
                mm.then_inc(ht_ready[h], 1)

            def layer1(g, h):
                first, n = HALVES[h]
                pe.wait_ge(smT_ready[h], g + 1)
                pe.wait_ge(h2T_ready[h], g + 1)
                if later(g):
                    pe.wait_ge(a1_ready[h], g)
                o = pM[:, 2 + h, 0:n * P].rearrange("p (j q) -> p j q", j=n)
                pe.matmul(o, w1[:, 0, :], hT[:, first:first + n, :], start=True, stop=False)
                pe.matmul(o, w1[:, 1, :], smT[:, first:first + n, :], start=False, stop=True
                          ).then_inc(l1_ready[h], 1)

            def layer2(g, h):
                first, n = HALVES[h]
                pe.wait_ge(a1_ready[h], g + 1)
                if later(g) or h:
                    pe.wait_ge(a2_ready, g * 2 + h)
                pe.matmul(pH[:, 0:n * P].rearrange("p (j q) -> p j q", j=n), w2[:], a1[:, first:first + n, :],
                          start=True, stop=True).then_inc(l2_ready, 1)

            def layer3(g, h):
                first, n = HALVES[h]
                if later(g) or h:
                    pe.wait_ge(o_ready, g * 2 + h)
                pe.matmul(pO[:, 0:n * P], ones_b[:], b3_rows[:, 0:n * P], start=True, stop=False,
                          skip_group_check=True)
                pe.wait_ge(a2_ready, g * 2 + h + 1)
                for j in range(n):
                    mm = pe.matmul(pO[:, j * P:(j + 1) * P], a2[:, first + j, :], w3[:], start=False,
                                   stop=(j == n - 1), skip_group_check=True)
                mm.then_inc(l3_ready, 1)

            def pe_tick(g, h):
                for stage, ahead in ((turn, 0), (layer3, -2), (layer2, -1), (layer1, 0)):
                    at = unit(g, h, ahead, NG)
                    if at:
                        stage(*at)

            for tick in range(-2, 2 * NG + 2):
                pe_tick(tick // 2, tick % 2)

        @block.vector
        def _(dve):
            dve.memset(dst_t[96:P, LAST:STEPS], PAD_DST).then_inc(pad_set, 1)
            dve.memset(src_t[96:P, LAST:STEPS], 0).then_inc(pad_set, 1)
            dve.memset(X[96:P, FULL_T, :], 0.0).then_inc(pad_set, 1)
            dve.memset(prev_i[:], -1).then_inc(pad_set, 1)
            dve.memset(b3_f[:], 0.0).then_inc(pad_set, 1)
            dve.memset(eps_col[:], EPS).then_inc(dve_own, 1)
            dve.memset(no_edges_row[:, 0:D], -BIG).then_inc(none_set, 1)
            dve.memset(no_edges_row[:, D:2 * D], 0.0).then_inc(none_set, 1)
            dve.memset(zeros_b[:], 0.0).then_inc(init_set, 1)
            dve.memset(run[:, SLOTS - 1, CHUNK - 1, 0:D], -BIG).then_inc(dve_own, 1)
            dve.memset(run[:, SLOTS - 1, CHUNK - 1, D:2 * D], 0.0).then_inc(dve_own, 1)
            dve.memset(runT[:, :, 0:1], 0.0).then_inc(dve_own, 1)
            dve.wait_ge(const_set, 5)
            dve.tensor_copy(iota_b[:], iota_i[:]).then_inc(dve_own, 1)
            dve.tensor_copy(part_f[:], part_i[:]).then_inc(dve_own, 1)

            def weights():
                dve.wait_ge(w0_turned, 1)
                dve.tensor_copy(w0T[:, 0:D], pO[:, P:2 * P]).then_inc(w0_ready, 1)
                dve.wait_ge(w0_ready, 1)
                dve.tensor_tensor(w0T[:, D:2 * D], pO[:, 0:P], w0T[:, 0:D], ALU.subtract).then_inc(w0_ready, 1)

            def statistics(g):
                dve.wait_ge(x_in[g], 32 if g == NG - 1 else 16)
                for t in range(g * GROUP, (g + 1) * GROUP):
                    ins = dve.bn_stats(stats[:, t, :], X[:, t, :])
                ins.then_inc(stat_own, 1)
                dve.wait_ge(stat_own, g + 1)
                for t in range(g * GROUP, (g + 1) * GROUP):
                    ins = dve.bn_aggr(mv[:, t, :], stats[:, t, :])
                ins.then_inc(var1_ready, 1)

            def scale(g):
                ts = slice(g * GROUP, (g + 1) * GROUP)
                dve.wait_ge(std1_ready, g + 1)
                dve.reciprocal(rstd[:, ts], std[:, ts]).then_inc(stat_ready, 1)

            def take_B(g):
                first, n = HALVES[0]
                ts = slice(g * GROUP + first, g * GROUP + first + n)
                dve.wait_ge(stat_ready, g + 1)
                dve.wait_ge(b_ready[0], g + 1)
                dve.tensor_tensor(AB[:, ts, 0:D], by_tile(pM[:, 0], 0),
                                  rstd[:, ts].rearrange("p (t a) -> p t a", a=1).to_broadcast([P, n, D]), ALU.mult
                                  ).then_inc(b_taken[0], 1)

            for g in range(NG):
                statistics(g)
                if g == 0:
                    weights()
                if g >= 1:
                    scale(g - 1)
                if g >= 3:
                    take_B(g - 3)
            scale(NG - 1)
            take_B(NG - 3)
            take_B(NG - 2)
            take_B(NG - 1)
            own = 6

            dve.wait_ge(dst_in, 64)
            dve.tensor_copy(dst_f[:], dst_t[:]).then_inc(dve_own, 1)
            dve.tensor_copy(prev_f[:], prev_i[:]).then_inc(dve_own, 1)
            dve.tensor_scalar(tmp_i[:], dst_t[:], 7, None, ALU.logical_shift_right).then_inc(dve_own, 1)
            dve.wait_ge(dve_own, own + 3)
            dve.tensor_copy(hi_b[:], tmp_i[:]).then_inc(dve_own, 1)
            dve.tensor_scalar(drop[:], dst_f[:], dst_f[:, 0:1], None, ALU.is_equal).then_inc(dve_own, 1)
            dve.tensor_scalar(cont[:], prev_f[:], dst_f[:, 0:1], None, ALU.is_equal).then_inc(dve_own, 1)
            dve.wait_ge(dve_own, own + 6)
            dve.tensor_scalar(tmp_i[:], dst_t[:], P - 1, None, ALU.bitwise_and).then_inc(dve_own, 1)
            dve.tensor_reduce(first_n[:], drop[:], mybir.AxisListType.X, ALU.add).then_inc(dve_own, 1)
            dve.memset(keep[:, 0:1], 0.0).then_inc(dve_own, 1)
            dve.tensor_tensor(keep[:, 1:STEPS], dst_f[:, 1:STEPS], dst_f[:, 0:STEPS - 1], ALU.is_equal
                              ).then_inc(dve_own, 1)
            dve.wait_ge(dve_own, own + 10)
            dve.tensor_copy(lo_b[:], tmp_i[:]).then_inc(dve_own, 1)
            dve.tensor_scalar(drop[:], keep[:], 1.0, BIG, ALU.subtract, ALU.mult).then_inc(dve_own, 1)
            dve.scalar_tensor_tensor(out=fix_f[:], in0=first_n[:], scalar=-1.0, in1=part_f[:], op0=ALU.add,
                                     op1=ALU.add).then_inc(dve_own, 1)
            dve.tensor_scalar(through[:], first_n[:], float(STEPS), cont[:, 0:1], ALU.is_equal, ALU.mult
                              ).then_inc(dve_own, 1)
            dve.tensor_scalar(cont_neg[:], cont[:], 1.0, BIG, ALU.subtract, ALU.mult).then_inc(dve_own, 1)
            dve.wait_ge(dve_own, own + 15)
            dve.tensor_copy(fix_i[:], fix_f[:]).then_inc(fix_ready, 1)
            dve.tensor_scalar(diag[:], ident[:], through[:, 0:1], None, ALU.mult).then_inc(diag_ready, 1)
            own += 15
            dve.wait_ge(u_ready, 1)
            dve.tensor_tensor(c1_col[:], pO[:, 256:257], b1_col[:], ALU.add).then_inc(c1_ready, 1)
            dve.wait_ge(w_in, 16 * 10)
            dve.memset(b3_rows[:], 0.0).then_inc(dve_own, 1)
            dve.memset(ones_b[:], 1.0).then_inc(dve_own, 1)
            own += 2
            for m in range(3):
                dve.tensor_copy(b3_part[:], b3_f[:]).then_inc(dve_own, 1)
                dve.wait_ge(dve_own, own + 1)
                row = slice(32 * m, 32 * m + 1)
                dve.tensor_copy(b3_rows[row, :], b3_part[row, :]).then_inc(dve_own, 1)
                dve.tensor_tensor(b3_f[:], b3_f[:], b3_part[:], ALU.subtract).then_inc(dve_own, 1)
                dve.wait_ge(dve_own, own + 3)
                own += 3
            dve.wait_ge(thr_ready, 1)
            dve.tensor_copy(thr_row[:, 1, :], pT[:, 1, 0:P]).then_inc(dve_own, 1)
            dve.tensor_scalar(thr_row[:, 0, :], pT[:, 1, 0:P], 1.0, BIG, ALU.subtract, ALU.mult).then_inc(dve_own, 1)
            own += 2
            dve.wait_ge(a_taken[0], NG)
            dve.wait_ge(a_taken[1], NG)
            dve.tensor_tensor(A, A, b0_rows[:].rearrange("p (a d) -> p a d", a=1).to_broadcast([P, NT, D]),
                              ALU.add).then_inc(dve_own, 1)
            own += 1

            def chunk(i, s, last=False):
                k0 = i * (SLOTS * CHUNK) + s * CHUNK
                if later(i):
                    dve.wait_ge(counted[s], i)
                dve.tensor_tensor(
                    oh_lo[:, s], iota_b[:].rearrange("p (a q) -> p a q", a=1).to_broadcast([P, CHUNK, P]),
                    lo_b[:, bass.ds(k0, CHUNK)].rearrange("p (k a) -> p k a", a=1).to_broadcast([P, CHUNK, P]),
                    ALU.is_equal).then_inc(onehots[s], 1)
                dve.tensor_tensor(
                    oh_hi[:, s], iota_b[:, 0:NT].rearrange("p (a q) -> p a q", a=1).to_broadcast([P, CHUNK, NT]),
                    hi_b[:, bass.ds(k0, CHUNK)].rearrange("p (k a) -> p k a", a=1).to_broadcast([P, CHUNK, NT]),
                    ALU.is_equal).then_inc(onehots[s], 1)
                if not last:
                    dve.wait_ge(gathered[s], i * (16 * CHUNK) + 16 * CHUNK)
                dve.wait_ge(attr_in[s], i * 48 + 48)
                if later(i):
                    dve.wait_ge(rows_out[s], i * 16)
                for j in range(CHUNK):
                    to = run[:, s, j]
                    was = run[:, s, j - 1] if j else run[:, (s - 1) % SLOTS, CHUNK - 1]
                    if last:
                        dve.wait_ge(last_gathered[j], 16)
                    if j:
                        dve.wait_ge(max_steps, i * (SLOTS * (CHUNK - 1)) + s * (CHUNK - 1) + j)
                    else:
                        if later(i) or s:
                            dve.wait_ge(max_done[s - 1], i + 1 if s else i)
                    ins = dve.scalar_tensor_tensor(
                        out=to[:, 0:D], in0=was[:, 0:D], scalar=drop[:, bass.ds(k0 + j, 1)],
                        in1=gat[:, s, j, :], op0=ALU.add, op1=ALU.max)
                    if j < CHUNK - 1:
                        ins.then_inc(max_steps, 1)
                    else:
                        ins.then_inc(max_done[s], 1)
                    if j:
                        dve.wait_ge(sum_steps, i * (SLOTS * (CHUNK - 1)) + s * (CHUNK - 1) + j)
                    else:
                        if later(i) or s:
                            dve.wait_ge(sum_done[s - 1], i + 1 if s else i)
                    ins = dve.scalar_tensor_tensor(
                        out=to[:, D:2 * D], in0=was[:, D:2 * D], scalar=keep[:, bass.ds(k0 + j, 1)],
                        in1=att[:, s, j, :], op0=ALU.mult, op1=ALU.add)
                    if j < CHUNK - 1:
                        ins.then_inc(sum_steps, 1)
                    else:
                        ins.then_inc(sum_done[s], 1)

            for i in peeled(dve, LOOPS - 1):
                for s in range(SLOTS):
                    chunk(i, s)
            for s in range(SLOTS):
                chunk(LOOPS - 1, s, last=s == SLOTS - 1)

            dve.wait_ge(carry_turned, 1)
            dve.wait_ge(dve_own, own)
            dve.tensor_tensor_scan(out=runT[:, 0, 1:P + 1], data0=thr_row[:, 0, :], data1=pT[:, 0, 0:P],
                                   initial=-BIG, op0=ALU.add, op1=ALU.max).then_inc(run_ready, 1)
            dve.tensor_tensor_scan(out=runT[:, 1, 1:P + 1], data0=thr_row[:, 1, :], data1=pT[:, 0, P:2 * P],
                                   initial=0.0, op0=ALU.mult, op1=ALU.add).then_inc(run_ready, 1)

            dve.wait_ge(hist_done, 1)
            dve.tensor_copy(count[:], pH[:, 0:NT]).then_inc(count_ready, 1)
            dve.wait_ge(prefix_ready, 1)
            dve.wait_ge(count_ready, 1)
            dve.tensor_scalar(has[:], count[:], 0.5, None, ALU.is_gt).then_inc(dve_own, 1)
            dve.tensor_copy(tot[:], pO[:, NT:2 * NT]).then_inc(dve_own, 1)
            dve.wait_ge(dve_own, own + 2)
            dve.memset(end_f[:], 0.0).then_inc(dve_own, 1)
            dve.wait_ge(dve_own, own + 3)
            dve.tensor_tensor_scan(out=totscan[:], data0=tot[:], data1=end_f[:], initial=0.0, op0=ALU.add,
                                   op1=ALU.add).then_inc(dve_own, 1)
            dve.wait_ge(dve_own, own + 4)
            dve.tensor_tensor(end_f[:], totscan[:], tot[:], ALU.subtract).then_inc(dve_own, 1)
            dve.wait_ge(dve_own, own + 5)
            dve.scalar_tensor_tensor(out=totscan[:], in0=pO[:, 0:NT], scalar=-1.0 - NO_EDGES, in1=end_f[:],
                                     op0=ALU.add, op1=ALU.add).then_inc(dve_own, 1)
            dve.wait_ge(dve_own, own + 6)
            dve.tensor_tensor(end_f[:], totscan[:], has[:], ALU.mult).then_inc(dve_own, 1)
            dve.wait_ge(dve_own, own + 7)
            dve.tensor_scalar(end_i[:], end_f[:], float(NO_EDGES), None, ALU.add).then_inc(end_ready, 1)
            own += 7

            dve.wait_ge(run_turned, 1)
            dve.wait_ge(fix_in, 16)
            dve.scalar_tensor_tensor(out=fix[:, 0:D], in0=pM[:, 0, 0:P], scalar=cont_neg[:, 0:1], in1=fix[:, 0:D],
                                     op0=ALU.add, op1=ALU.max).then_inc(fix_ready, 1)
            dve.scalar_tensor_tensor(out=fix[:, D:2 * D], in0=pM[:, 0, P:2 * P], scalar=cont[:, 0:1],
                                     in1=fix[:, D:2 * D], op0=ALU.mult, op1=ALU.add).then_inc(fix_ready, 1)

            def own_before(g, h):
                return own + (g * 2 + h) * 3

            def message(g, h):
                first, n = HALVES[h]
                dve.wait_ge(end_in[h], g * (16 * n) + 16 * n)
                dve.tensor_tensor(z[:, first:first + n, :], tiles(ends, g, h)[:, :, 0:D], tiles(A, g, h), ALU.add
                                  ).then_inc(dve_own, 1)

            def residual(g, h):
                first, n = HALVES[h]
                dve.wait_ge(dve_own, own_before(g, h) + 1)
                dve.scalar_tensor_tensor(out=tiles(X, g, h), in0=z[:, first:first + n, :], scalar=0.0,
                                         in1=tiles(X, g, h), op0=ALU.max, op1=ALU.add).then_inc(dve_own, 1)

            def statistics2(g, h):
                first, n = HALVES[h]
                dve.wait_ge(dve_own, own_before(g, h) + 2)
                if later(g):
                    dve.wait_ge(h2_ready[h], g)
                dve.nop(nofuse=True)
                for j in range(first, first + n):
                    ins = dve.bn_stats(stats[:, j, :], X[:, bass.ds(g * GROUP + j, 1), :])
                ins.then_inc(dve_own, 1)
                dve.wait_ge(dve_own, own_before(g, h) + 3)
                dve.nop(nofuse=True)
                for j in range(first, first + n):
                    ins = dve.bn_aggr(mv[:, j, :], stats[:, j, :])
                ins.then_inc(var_ready[h], 1)

            def reciprocal2(g, h):
                first, n = HALVES[h]
                dve.wait_ge(std_ready, g * 2 + h + 1)
                dve.reciprocal(rstd[:, first:first + n], std[:, first:first + n]).then_inc(rstd2_ready, 1)

            def shift2(g, h):
                first, n = HALVES[h]
                ts = slice(first, first + n)
                dve.wait_ge(rstd2_ready, g * 2 + h + 1)
                dve.scalar_tensor_tensor(out=nmr[:, ts], in0=mv[:, ts, 0], scalar=-1.0, in1=rstd[:, ts],
                                         op0=ALU.mult, op1=ALU.mult).then_inc(x1_ready[h], 1)

            def take_h_turned(g, h):
                if h:
                    return
                first, n = HALVES[h]
                dve.wait_ge(ht_ready[h], g + 1)
                if later(g):
                    dve.wait_ge(l1_ready[h], g)
                dve.tensor_copy(hT[:, first:first + n, :], pT[:, h, 0:n * P].rearrange("p (j q) -> p j q", j=n)
                                ).then_inc(h2T_ready[h], 1)

            def result(g, h):
                first, n = HALVES[h]
                dve.wait_ge(l3_ready, g * 2 + h + 1)
                if later(g):
                    dve.wait_ge(o_out[h], g * 16)
                dve.tensor_tensor(ost[:, first:first + n, :], pO[:, 0:n * P].rearrange("p (j q) -> p j q", j=n),
                                  tiles(X, g, h), ALU.add).then_inc(o_ready, 1)

            def dve_tick(g, h):
                for stage, ahead in ((reciprocal2, 1), (shift2, 1), (take_h_turned, 0), (message, 2),
                                     (result, -2), (residual, 2), (statistics2, 2)):
                    at = unit(g, h, ahead, NG)
                    if at:
                        stage(*at)

            pipeline(dve, NG, dve_tick, 2, 2)


_NAMES = ['x', 'src', 'dst', 'edge_attr_128', 'L0_gnn_W', 'L0_gnn_b', 'L1_gnn_u', 'L1_gnn_W1', 'L1_gnn_b1',
          'L1_gnn_W2', 'L1_gnn_b2', 'L1_gnn_W3', 'L1_gnn_b3']


def kernel(**inputs):
    import concourse.bacc as bacc
    from concourse.bass_utils import run_bass_kernel_spmd

    nc = bacc.Bacc("TRN2", target_bir_lowering=False, num_devices=1)
    arrays = {f"{n}_dram": np.ascontiguousarray(inputs[n]) for n in _NAMES}
    args = [nc.dram_tensor(n, a.shape, mybir.dt.from_np(a.dtype), kind="ExternalInput").ap()
            for n, a in arrays.items()]
    out = nc.dram_tensor("out_dram", tuple(inputs['x'].shape), F32, kind="ExternalOutput").ap()
    gnn_block(nc, *args, out)
    return run_bass_kernel_spmd(nc, [arrays], core_ids=[0]).results[0]["out_dram"]
```
